# Optimizing a Trainium2 kernel written in Bass

```python
import numpy as np
import jax
import jax.numpy as jnp

def _softmax(x, axis=-1):
    return jax.nn.softmax(x, axis=axis)

def _gelu(x):
    return jax.nn.gelu(x, approximate=True)

def _silu(x):
    return jax.nn.silu(x)

def _sigmoid(x):
    return jax.nn.sigmoid(x)

def _layernorm(x, axis=-1, eps=1e-05):
    m = jnp.mean(x, axis=axis, keepdims=True)
    v = jnp.var(x, axis=axis, keepdims=True)
    return (x - m) / jnp.sqrt(v + eps)

def _scatter_add(tgt, idx, src, axis=0):
    return tgt.at[idx].add(src)

def _segment_sum(src, seg, n):
    return jax.ops.segment_sum(src, seg, n)
kernel_name = 'mk_flamingo_gated_d2_seqx_r8_9032a4'

def setup_inputs(seed: int=0):
    np.random.seed(seed)
    _w = jnp.asarray

    def _rec_inputs():
        import jax
        import jax.numpy as jnp
        _rk = jax.random.key(seed)
        x = -0.0002928 + 1 * jax.random.normal(jax.random.fold_in(_rk, 1), (64, 64, 256), jnp.float32)
        _lenS = 64 - jax.random.randint(jax.random.fold_in(_rk, 7), (64,), 0, max(1, 64 // 4) + 1, jnp.int32)
        _lenS2 = 64 - jax.random.randint(jax.random.fold_in(_rk, 8), (64,), 0, max(1, 64 // 4) + 1, jnp.int32)
        _ctx_2048P = jax.random.normal(jax.random.fold_in(_rk, 11), (64, 16, 256), jnp.float32)
        _ctx_2048c = jax.random.dirichlet(jax.random.fold_in(_rk, 511), 0.3 * jnp.ones((16,), jnp.float32), (64, 64))
        _ctx_2048t = jnp.einsum('bsk,bkd->bsd', _ctx_2048c, _ctx_2048P)
        _ctx_2048t = _ctx_2048t * jax.lax.rsqrt(jnp.mean(jnp.square(_ctx_2048t)) + 1e-12) * 0.953939
        ctx_2048 = -1.39393e-06 + 0.999914 * (_ctx_2048t + 0.3 * jax.random.normal(jax.random.fold_in(_rk, 611), (64, 64, 256), jnp.float32))
        _g = jax.random.normal(jax.random.fold_in(_rk, 9001), (2, 2), jnp.float32)
        _g = jnp.sign(_g) * jnp.maximum(jnp.abs(_g), 1.0) + (_g == 0) * 1.0
        g_xattn = _g[0]
        g_ffn = _g[1]
        return (x, ctx_2048, g_xattn, g_ffn)
    x, ctx_2048, g_xattn, g_ffn = _rec_inputs()

    def _L0_xattn_setup():
        import jax, jax.numpy as jnp
        import numpy as np
        N_HEADS = 8
        ROPE_BASE = 10000.0

        def _rope(x, d):
            t = x.shape[2]
            theta = 1.0 / ROPE_BASE ** (jnp.arange(0, d, 2, dtype=jnp.float32) / d)
            idx = jnp.arange(t, dtype=jnp.float32)[:, None] * theta[None, :]
            idx2 = jnp.concatenate([idx, idx], axis=-1)
            cos = jnp.cos(idx2)[None, None, :, :]
            sin = jnp.sin(idx2)[None, None, :, :]
            x_rope, x_pass = (x[..., :d], x[..., d:])
            d2 = d // 2
            neg_half = jnp.concatenate([-x_rope[..., d2:], x_rope[..., :d2]], axis=-1)
            x_rope = x_rope * cos + neg_half * sin
            return jnp.concatenate([x_rope, x_pass], axis=-1)

        def _proj(W, b, x):
            return jnp.einsum('oc,bct->bot', W, x) + b[None, :, None]
        key = jax.random.key(seed)
        ks = jax.random.split(key, 12)
        B, CH, T = (4, 64, 256)
        s = 1.0 / np.sqrt(CH)
        return {'x': jax.random.normal(ks[0], (B, CH, T), jnp.float32), 'c': jax.random.normal(ks[1], (B, CH, T), jnp.float32), 'Wq': jax.random.normal(ks[2], (CH, CH), jnp.float32) * s, 'bq': jax.random.normal(ks[3], (CH,), jnp.float32) * 0.01, 'Wk': jax.random.normal(ks[4], (CH, CH), jnp.float32) * s, 'bk': jax.random.normal(ks[5], (CH,), jnp.float32) * 0.01, 'Wv': jax.random.normal(ks[6], (CH, CH), jnp.float32) * s, 'bv': jax.random.normal(ks[7], (CH,), jnp.float32) * 0.01, 'Wo': jax.random.normal(ks[8], (CH, CH), jnp.float32) * s, 'bo': jax.random.normal(ks[9], (CH,), jnp.float32) * 0.01}
    _L0_xattn_all = _L0_xattn_setup()
    _L0_xattn_in = {k: v for k, v in _L0_xattn_all.items() if k in ('Wq', 'bq', 'Wk', 'bk', 'Wv', 'bv', 'Wo', 'bo')}
    del _L0_xattn_all

    def _L0_ffn_setup():
        import jax, jax.numpy as jnp
        import numpy as np
        from jax import lax
        E = 8
        K = 2
        H = 256
        I = 512
        B, S = (2, 256)
        SCALE = 0.02

        def _silu_and_mul(gu):
            g, u = jnp.split(gu, 2, axis=-1)
            return jax.nn.silu(g) * u
        key = jax.random.key(seed)
        ks = jax.random.split(key, 6)
        return {'hidden_states': jax.random.normal(ks[0], (B, S, H), dtype=jnp.float32), 'gate_w': jax.random.normal(ks[1], (H, E), dtype=jnp.float32) * SCALE, 'w_gate_up': jax.random.normal(ks[2], (E, H, 2 * I), dtype=jnp.float32) * SCALE, 'w_down': jax.random.normal(ks[3], (E, I, H), dtype=jnp.float32) * SCALE, 'shared_gate_up': jax.random.normal(ks[4], (H, 2 * I), dtype=jnp.float32) * SCALE, 'shared_down': jax.random.normal(ks[5], (I, H), dtype=jnp.float32) * SCALE}
    _L0_ffn_all = _L0_ffn_setup()
    _L0_ffn_in = {k: v for k, v in _L0_ffn_all.items() if k in ('gate_w', 'w_gate_up', 'w_down', 'shared_gate_up', 'shared_down')}
    del _L0_ffn_all

    def _L1_xattn_setup():
        import jax, jax.numpy as jnp
        import numpy as np
        NUM_HEADS = 8
        MODEL_DIM = 256
        MAX_SQRT_GRADIENT = 1000.0

        @jax.custom_vjp
        def sqrt_bound_derivative(x):
            return jnp.sqrt(x)

        def _sbd_fwd(x):
            return (jnp.sqrt(x), x)

        def _sbd_bwd(x, g):
            return (g / (2.0 * jnp.sqrt(jnp.clip(x, 1.0 / MAX_SQRT_GRADIENT ** 2, None))),)
        sqrt_bound_derivative.defvjp(_sbd_fwd, _sbd_bwd)

        def block_diag_linear(x, w, b):
            B, T, D = x.shape
            H = w.shape[0]
            xh = x.reshape(B, T, H, D // H)
            y = jnp.einsum('bthi,hij->bthj', xh, w) + b
            return y.reshape(B, T, D)

        def self_att_pool(h, num_heads):
            B, T, D = h.shape
            dh = D // num_heads
            hh = h.reshape(B, T, num_heads, dh)
            logits = hh.mean(axis=-1)
            attn = jax.nn.softmax(logits, axis=1)
            pooled = jnp.einsum('bth,bthd->bhd', attn, hh)
            return pooled.reshape(B, 1, D)
        key = jax.random.key(seed)
        ks = jax.random.split(key, 8)
        B, T, D, H = (2, 1024, MODEL_DIM, NUM_HEADS)
        dh = D // H
        x = jax.random.normal(ks[0], (B, T, D), dtype=jnp.float32)
        h = jax.random.normal(ks[1], (B, T, D), dtype=jnp.float32)
        scale = 1.0 / np.sqrt(dh)
        w_input = jax.random.normal(ks[2], (H, dh, dh), dtype=jnp.float32) * scale
        b_input = jnp.zeros((H, dh), dtype=jnp.float32)
        w_a = jax.random.normal(ks[3], (H, dh, dh), dtype=jnp.float32) * scale
        b_a = jnp.zeros((H, dh), dtype=jnp.float32)
        u = jax.random.uniform(ks[4], (D,), minval=0.9 ** 2, maxval=0.999 ** 2)
        r = jnp.sqrt(u)
        y = -jnp.log(r) / 8.0
        a_param = jnp.log(jnp.expm1(y)).astype(jnp.float32)
        return {'x': x, 'h': h, 'w_input': w_input, 'b_input': b_input, 'w_a': w_a, 'b_a': b_a, 'a_param': a_param}
    _L1_xattn_all = _L1_xattn_setup()
    _L1_xattn_in = {k: v for k, v in _L1_xattn_all.items() if k in ('w_input', 'b_input', 'w_a', 'b_a', 'a_param')}
    del _L1_xattn_all

    def _L1_ffn_setup():
        import jax, jax.numpy as jnp
        import numpy as np
        B, S, D, H = (4, 256, 256, 1024)

        def fwht(x):
            orig_shape = x.shape
            n = orig_shape[-1]
            x = x.reshape(-1, n)
            h = 1
            while h < n:
                xb = x.reshape(-1, n // (2 * h), 2, h)
                a = xb[:, :, 0, :]
                b = xb[:, :, 1, :]
                x = jnp.stack([a + b, a - b], axis=2).reshape(-1, n)
                h *= 2
            scale = jnp.asarray(1.0 / np.sqrt(n), dtype=x.dtype)
            return (x * scale).reshape(orig_shape)
        key = jax.random.key(seed)
        kx, k1, k2, k3 = jax.random.split(key, 4)
        x = jax.random.normal(kx, (B, S, D), dtype=jnp.float32)
        W1 = jax.random.normal(k1, (H, D), dtype=jnp.float32) * (1.0 / np.sqrt(D))
        W2 = jax.random.normal(k2, (D, H), dtype=jnp.float32) * (1.0 / np.sqrt(H))
        W3 = jax.random.normal(k3, (H, D), dtype=jnp.float32) * (1.0 / np.sqrt(D))
        return {'x': x, 'W1': W1, 'W2': W2, 'W3': W3}
    _L1_ffn_all = _L1_ffn_setup()
    _L1_ffn_in = {k: v for k, v in _L1_ffn_all.items() if k in ('W1', 'W2', 'W3')}
    del _L1_ffn_all
    return {'x': x, 'ctx_2048': ctx_2048, 'g_xattn': g_xattn, 'g_ffn': g_ffn, 'L0_xattn_Wq': _L0_xattn_in['Wq'], 'L0_xattn_bq': _L0_xattn_in['bq'], 'L0_xattn_Wk': _L0_xattn_in['Wk'], 'L0_xattn_bk': _L0_xattn_in['bk'], 'L0_xattn_Wv': _L0_xattn_in['Wv'], 'L0_xattn_bv': _L0_xattn_in['bv'], 'L0_xattn_Wo': _L0_xattn_in['Wo'], 'L0_xattn_bo': _L0_xattn_in['bo'], 'L0_ffn_gate_w': _L0_ffn_in['gate_w'], 'L0_ffn_w_gate_up': _L0_ffn_in['w_gate_up'], 'L0_ffn_w_down': _L0_ffn_in['w_down'], 'L0_ffn_shared_gate_up': _L0_ffn_in['shared_gate_up'], 'L0_ffn_shared_down': _L0_ffn_in['shared_down'], 'L1_xattn_w_input': _L1_xattn_in['w_input'], 'L1_xattn_b_input': _L1_xattn_in['b_input'], 'L1_xattn_w_a': _L1_xattn_in['w_a'], 'L1_xattn_b_a': _L1_xattn_in['b_a'], 'L1_xattn_a_param': _L1_xattn_in['a_param'], 'L1_ffn_W1': _L1_ffn_in['W1'], 'L1_ffn_W2': _L1_ffn_in['W2'], 'L1_ffn_W3': _L1_ffn_in['W3']}

def reference(x, ctx_2048, g_xattn, g_ffn, L0_xattn_Wq, L0_xattn_bq, L0_xattn_Wk, L0_xattn_bk, L0_xattn_Wv, L0_xattn_bv, L0_xattn_Wo, L0_xattn_bo, L0_ffn_gate_w, L0_ffn_w_gate_up, L0_ffn_w_down, L0_ffn_shared_gate_up, L0_ffn_shared_down, L1_xattn_w_input, L1_xattn_b_input, L1_xattn_w_a, L1_xattn_b_a, L1_xattn_a_param, L1_ffn_W1, L1_ffn_W2, L1_ffn_W3):
    import jax
    import jax.numpy as jnp

    def _L0_xattn_ref(x, c, Wq, bq, Wk, bk, Wv, bv, Wo, bo):
        import jax, jax.numpy as jnp
        import numpy as np
        N_HEADS = 8
        ROPE_BASE = 10000.0

        def _rope(x, d):
            t = x.shape[2]
            theta = 1.0 / ROPE_BASE ** (jnp.arange(0, d, 2, dtype=jnp.float32) / d)
            idx = jnp.arange(t, dtype=jnp.float32)[:, None] * theta[None, :]
            idx2 = jnp.concatenate([idx, idx], axis=-1)
            cos = jnp.cos(idx2)[None, None, :, :]
            sin = jnp.sin(idx2)[None, None, :, :]
            x_rope, x_pass = (x[..., :d], x[..., d:])
            d2 = d // 2
            neg_half = jnp.concatenate([-x_rope[..., d2:], x_rope[..., :d2]], axis=-1)
            x_rope = x_rope * cos + neg_half * sin
            return jnp.concatenate([x_rope, x_pass], axis=-1)

        def _proj(W, b, x):
            return jnp.einsum('oc,bct->bot', W, x) + b[None, :, None]
        b, ch, t_t = x.shape
        t_s = c.shape[2]
        h = N_HEADS
        kc = ch // h
        d_rope = int(kc * 0.5)
        q = _proj(Wq, bq, x)
        k = _proj(Wk, bk, c)
        v = _proj(Wv, bv, c)
        q = q.reshape(b, h, kc, t_t).transpose(0, 1, 3, 2)
        k = k.reshape(b, h, kc, t_s).transpose(0, 1, 3, 2)
        v = v.reshape(b, h, kc, t_s).transpose(0, 1, 3, 2)
        q = _rope(q, d_rope)
        k = _rope(k, d_rope)
        scores = jnp.einsum('bhqd,bhkd->bhqk', q, k) / jnp.sqrt(jnp.float32(kc))
        p_attn = jax.nn.softmax(scores, axis=-1)
        out = jnp.einsum('bhqk,bhkd->bhqd', p_attn, v)
        out = out.transpose(0, 1, 3, 2).reshape(b, ch, t_t)
        return _proj(Wo, bo, out)

    def _L0_ffn_ref(hidden_states, gate_w, w_gate_up, w_down, shared_gate_up, shared_down):
        import jax, jax.numpy as jnp
        import numpy as np
        from jax import lax
        E = 8
        K = 2
        H = 256
        I = 512
        B, S = (2, 256)
        SCALE = 0.02

        def _silu_and_mul(gu):
            g, u = jnp.split(gu, 2, axis=-1)
            return jax.nn.silu(g) * u
        orig_shape = hidden_states.shape
        x = hidden_states.reshape(-1, orig_shape[-1])
        shared_out = _silu_and_mul(x @ shared_gate_up) @ shared_down
        router_logits = x @ gate_w
        probs = jax.nn.softmax(router_logits, axis=-1)
        topk_w, topk_i = lax.top_k(probs, K)
        topk_w = topk_w / jnp.sum(topk_w, axis=-1, keepdims=True)
        combine = jnp.sum(jax.nn.one_hot(topk_i, E, dtype=x.dtype) * topk_w[..., None], axis=1)

        def body(acc, we):
            wg, wd, cw = we
            h = _silu_and_mul(x @ wg) @ wd
            return (acc + cw[:, None] * h, None)
        moe_out, _ = lax.scan(body, jnp.zeros_like(x), (w_gate_up, w_down, combine.T))
        return (moe_out + shared_out).reshape(orig_shape)

    def _L1_xattn_ref(x, h, w_input, b_input, w_a, b_a, a_param):
        import jax, jax.numpy as jnp
        import numpy as np
        NUM_HEADS = 8
        MODEL_DIM = 256
        MAX_SQRT_GRADIENT = 1000.0

        @jax.custom_vjp
        def sqrt_bound_derivative(x):
            return jnp.sqrt(x)

        def _sbd_fwd(x):
            return (jnp.sqrt(x), x)

        def _sbd_bwd(x, g):
            return (g / (2.0 * jnp.sqrt(jnp.clip(x, 1.0 / MAX_SQRT_GRADIENT ** 2, None))),)
        sqrt_bound_derivative.defvjp(_sbd_fwd, _sbd_bwd)

        def block_diag_linear(x, w, b):
            B, T, D = x.shape
            H = w.shape[0]
            xh = x.reshape(B, T, H, D // H)
            y = jnp.einsum('bthi,hij->bthj', xh, w) + b
            return y.reshape(B, T, D)

        def self_att_pool(h, num_heads):
            B, T, D = h.shape
            dh = D // num_heads
            hh = h.reshape(B, T, num_heads, dh)
            logits = hh.mean(axis=-1)
            attn = jax.nn.softmax(logits, axis=1)
            pooled = jnp.einsum('bth,bthd->bhd', attn, hh)
            return pooled.reshape(B, 1, D)
        gate_x = jax.nn.sigmoid(block_diag_linear(x, w_input, b_input))
        gate_a = jax.nn.sigmoid(block_diag_linear(x, w_a, b_a))
        log_a = -8.0 * jax.nn.softplus(a_param) * gate_a
        a = jnp.exp(log_a)
        gated_x = x * gate_x
        normalized_x = gated_x * sqrt_bound_derivative(1.0 - jnp.exp(2.0 * log_a))
        h_pooled = self_att_pool(h, NUM_HEADS)
        return a * h_pooled + normalized_x

    def _L1_ffn_ref(x, W1, W2, W3):
        import jax, jax.numpy as jnp
        import numpy as np
        B, S, D, H = (4, 256, 256, 1024)

        def fwht(x):
            orig_shape = x.shape
            n = orig_shape[-1]
            x = x.reshape(-1, n)
            h = 1
            while h < n:
                xb = x.reshape(-1, n // (2 * h), 2, h)
                a = xb[:, :, 0, :]
                b = xb[:, :, 1, :]
                x = jnp.stack([a + b, a - b], axis=2).reshape(-1, n)
                h *= 2
            scale = jnp.asarray(1.0 / np.sqrt(n), dtype=x.dtype)
            return (x * scale).reshape(orig_shape)
        up_gate = jnp.einsum('bsd,hd->bsh', x, W1)
        up_lin = jnp.einsum('bsd,hd->bsh', x, W3)
        hidden = jax.nn.silu(up_gate) * up_lin
        hidden = fwht(hidden)
        out = jnp.einsum('bsh,dh->bsd', hidden, W2)
        return out
    x = x + jnp.tanh(g_xattn[0]) * _L0_xattn_ref(_layernorm(x, axis=-1), ctx_2048, L0_xattn_Wq, L0_xattn_bq, L0_xattn_Wk, L0_xattn_bk, L0_xattn_Wv, L0_xattn_bv, L0_xattn_Wo, L0_xattn_bo)
    x = x + jnp.tanh(g_ffn[0]) * _L0_ffn_ref(_layernorm(x, axis=-1), L0_ffn_gate_w, L0_ffn_w_gate_up, L0_ffn_w_down, L0_ffn_shared_gate_up, L0_ffn_shared_down)
    x = x + jnp.tanh(g_xattn[1]) * _L1_xattn_ref(_layernorm(x, axis=-1), ctx_2048, L1_xattn_w_input, L1_xattn_b_input, L1_xattn_w_a, L1_xattn_b_a, L1_xattn_a_param)
    x = x + jnp.tanh(g_ffn[1]) * _L1_ffn_ref(_layernorm(x, axis=-1), L1_ffn_W1, L1_ffn_W2, L1_ffn_W3)
    return x

_drawn_inputs = setup_inputs


def setup_inputs(seed=0):
    import zlib

    import numpy as np

    out = dict(_drawn_inputs(seed))
    spreads = {'g_ffn': (-1.0, 0.6), 'L1_xattn_b_input': (0.0, 2.0), 'L1_xattn_b_a': (0.0, 2.0)}
    factors = {'L0_xattn_bq': 8.0,
     'L0_xattn_bk': 8.0,
     'L0_xattn_bv': 8.0,
     'L0_xattn_bo': 7.976,
     'L0_ffn_gate_w': 5.289,
     'L0_ffn_w_gate_up': 4.575,
     'L0_ffn_w_down': 4.583,
     'L0_ffn_shared_gate_up': 3.288,
     'L0_ffn_shared_down': 3.281,
     'L1_xattn_w_input': 22.104,
     'L1_xattn_w_a': 35.08,
     'L1_xattn_a_param': 23.928}
    for name, (base, spread) in spreads.items():
        noise = np.random.default_rng([zlib.crc32(name.encode()), seed]).standard_normal(out[name].shape)
        drawn = base * np.exp(spread * noise) if base else spread * noise
        out[name] = jnp.asarray(drawn.astype(out[name].dtype))
    for name, factor in factors.items():
        out[name] = (out[name] * factor).astype(out[name].dtype)
    return out
```

```python
from contextlib import ExitStack

import numpy as np

import concourse.bass as bass
from concourse import mybir

F32 = mybir.dt.float32
F32R = mybir.dt.float32r
ACT = mybir.ActivationFunctionType
ALU = mybir.AluOpType
AX_X = mybir.AxisListType.X

P = 128
BATCH, CH, D = 64, 64, 256
TILES = BATCH * CH // P
HEADS, DH = 8, 8
UNITS, UH = 4, 4
EXPERTS, FF = 8, 512
FF2 = 1024
GROUP = 512
GT = GROUP // P
GROUPS = BATCH * CH // GROUP
EPS = 1e-5
RING = 4


def column_order():
    j, d, u = np.meshgrid(range(UH), range(DH), range(UNITS), indexing="ij")
    return (u // 2).ravel(), ((u % 2 * UH + j) * DH + d).ravel(), d.ravel()


def rotary_tables():
    theta = np.float32(1.0) / np.float32(10000.0) ** (np.arange(0, 4, 2, dtype=np.float32) / np.float32(4))
    angle = np.arange(D, dtype=np.float32)[None, :] * theta[:, None].astype(np.float32)
    d = column_order()[2]
    rotated = (d < 4)[:, None]
    cos = np.where(rotated, np.cos(angle)[d % 2], 1).astype(np.float32)
    sin = np.where(rotated, np.where(d < 2, -1, 1)[:, None] * np.sin(angle)[d % 2], 0).astype(np.float32)
    return cos, sin


def wait_count(eng, sem, count):
    if not (isinstance(count, int) and count <= 0):
        eng.wait_ge(sem, count)


def wait_alone(eng):
    eng.nop(nofuse=True)


def attention(nc, dram, x, ident, tanh_gain):
    HP = 2 * HEADS
    LAG = 8
    ROWS, MROWS = 96, 104
    PEEL_FIRST, PEEL_LAST = (-2, -1, 0, 1), (30, 31, 32, 33)

    with ExitStack() as ctx:
        def sb(name, shape, dt=F32):
            return ctx.enter_context(nc.sbuf_tensor(name, shape, dt))

        def ps(name, shape, dt=F32):
            return ctx.enter_context(nc.psum_tensor(name, shape, dt))

        def sem(name):
            return nc.alloc_semaphore(name)

        w_in = sb("w_in", [P, 5, P])
        w_out = sb("w_out", [P, P])
        bias = sb("bias", [P, 5])
        bias_v = sb("bias_v", [P, P])
        rope = sb("rope", [P, 2, D])
        own_head = sb("own_head", [P, UH])
        out_bias = sb("out_bias", [P, 1])
        half = sb("half", [P, 1])

        c_in = [sb(f"c_in{r}", [P, D]) for r in range(RING)]
        stats = sb("stats", [P, 6])
        mean_var = sb("mean_var", [P, 2])
        var_eps = sb("var_eps", [P, 1])
        rstd = sb("rstd", [P, 1])
        xn = sb("xn", [P, D])
        roped = {a: sb(f"{a}_roped", [P, 2, D]) for a in "qk"}
        whole = {a: sb(f"{a}_whole", [P, D]) for a in "qk"}
        part = {a: sb(f"{a}_part", [P, 2, D], F32R) for a in "qk"}
        q_st = [sb(f"q_st{r}", [P, UNITS, D], F32R) for r in range(RING)]
        k_st = [sb(f"k_st{r}", [P, UNITS, UH, D], F32R) for r in range(RING)]
        v_st = [sb(f"v_st{r}", [P, 2, HP, 32]) for r in range(RING)]
        row_max = [sb(f"row_max{r}", [P, 2 * HP]) for r in range(2)]
        m_parts = sb("m_parts", [P, 4 * HP])
        m_rows = sb("m_rows", [4 * HP, P], F32R)
        e_t = [sb(f"e_t{r}", [P, 2, D]) for r in range(8)]
        o_sb = [sb(f"o_sb{r}", [P, 2, D]) for r in range(2)]
        o_rcp = sb("o_rcp", [P, HP])
        a_sb = sb("a_sb", [P, 2, 2, CH])
        a_t = sb("a_t", [P, D])
        y_sb = sb("y_sb", [P, D])

        s_ps = [ps(f"s_ps{r}", [P, 4, D]) for r in range(2)]
        st_ps = [ps(f"st_ps{r}", [P, 2, D]) for r in range(2)]
        o_ps = ps("o_ps", [P, 2, D])
        misc = ps("misc", [P, 512])

        consts_in = sem("consts_in")
        x_first_in, x_rest_in = sem("x_first_in"), sem("x_rest_in")
        c_loaded = [sem(f"c_loaded{r}") for r in range(RING)]
        q_stacked = [sem(f"q_stacked{r}") for r in range(RING)]
        k_stacked = [[sem(f"k_stacked{j}_{r}") for r in range(RING)] for j in range(UH // 2)]
        m_stacked = [sem(f"m_stacked{r}") for r in range(RING)]
        names = ("values_cleared first_cleared others_cleared ones_set own_set bias_ready half_set stats_raw stats_done eps_added rstd_ready xn_ready "
                 "q_projected q_roped q_summed q_high q_split k_projected k_roped k_summed k_high k_split "
                 "v_projected v_stored scored max_taken m_high m_split m_turned m_taken "
                 "st_scored exp_done pv_done o_taken o_turned rcp_ready o_normed a_turned a_taken "
                 "y_projected y_taken y_free").split()
        s = {name: sem(name) for name in names}

        def steps(eng, body, before_loop=None):
            for n in PEEL_FIRST:
                body(n, n, 0)
            if before_loop:
                before_loop()
            with eng.Fori(0, (PEEL_LAST[0] - PEEL_FIRST[-1] - 1) // RING) as i:
                for c in range(PEEL_FIRST[-1] + 1, PEEL_FIRST[-1] + 1 + RING):
                    body(i * RING + c, c, i)
            for n in PEEL_LAST:
                body(n, n, 0)

        def there(n, c, k):
            return not isinstance(n, int) or 0 <= n + k < TILES

        def uses(c, i, k):
            return i + (c + k) // RING + 1

        def st_head(s_):
            return (0, s_ - LAG) if s_ >= LAG else (-1, s_ + LAG)

        block = ctx.enter_context(nc.Block())

        @block.sync
        def _(sp):
            rows = dram["x"].rearrange("(n b) c t -> (b c) n t", b=2)
            sp.dma_start(x[:, 0:4, :], rows[:, 0:4, :]).then_inc(x_first_in, 16)
            for dst, src in ((w_in[:], dram["w_in"]), (w_out[:], dram["w_out"]), (bias[:], dram["bias"]),
                             (bias_v[:], dram["bias_v"]), (rope[:], dram["rope"]), (own_head[:], dram["own_head"])):
                sp.dma_start(dst, src).then_inc(consts_in, 16)
            ctx_rows = dram["ctx_2048"].rearrange("(n b) c t -> n (b c) t", b=2)

            def body(n, c, i):
                if there(n, c, 2):
                    r = (c + 2) % RING
                    wait_count(sp, s["v_projected"], n - 1)
                    sp.dma_start(c_in[r][:], ctx_rows[bass.ds(n + 2, 1), :, :] if not isinstance(n, int)
                                 else ctx_rows[n + 2:n + 3, :, :]).then_inc(c_loaded[r], 16)
                if isinstance(n, int) and n == -2:
                    for t in range(4, TILES, 14):
                        sp.dma_start(x[:, t:t + 14, :], rows[:, t:t + 14, :]).then_inc(x_rest_in, 16)
                if there(n, c, 0):
                    r = c % RING
                    sp.wait_ge(s["m_taken"], n + 1)
                    sp.dma_start(q_st[r][ROWS:MROWS, :, :].bitcast(F32),
                                 m_rows[:, :].bitcast(F32)).then_inc(m_stacked[r], 16)
                if there(n, c, 2):
                    r = (c + 2) % RING
                    wait_count(sp, s["st_scored"], HP * (n - 1))
                    wait_alone(sp)
                    sp.wait_ge(s["k_split"], n + 3)
                    if isinstance(n, int) and n == -2:
                        sp.wait_ge(s["first_cleared"], 2)
                        sp.wait_ge(s["others_cleared"], 2)
                    for j in range(UH):
                        for t, of in enumerate((0, 0, 1)):
                            sp.dma_start(k_st[r][32 * t + 8 * j:32 * t + 8 * j + 8, :, j, :].bitcast(F32),
                                         part["k"][32 * j:32 * j + 32, of, :].bitcast(F32))\
                                .then_inc(k_stacked[j // 2][r], 16)
                        if j == 1:
                            sp.wait_ge(s["q_split"], n + 3)
                            for t, of in enumerate((0, 1, 0)):
                                sp.dma_start(q_st[r][32 * t:32 * t + 32, :, :].bitcast(F32),
                                             part["q"][:, of, :].bitcast(F32)).then_inc(q_stacked[r], 16)

            steps(sp, body)

        @block.gpsimd
        def _(pool):
            nc.gpsimd.memset(half[:], -0.5).then_inc(s["half_set"], 1)
            nc.gpsimd.memset(y_sb[:], 0.0).then_inc(s["y_free"], 1)
            for r in (2, 3):
                nc.gpsimd.memset(k_st[r][0:ROWS, :, :, :].bitcast(F32), 0.0).then_inc(s["others_cleared"], 1)
            pool.wait_ge(s["half_set"], 1)

            def body(n, c, i):
                if there(n, c, 2):
                    pool.wait_ge(s["stats_done"], n + 3)
                    wait_count(pool, s["xn_ready"], n + 2)
                    wait_alone(pool)
                    nc.gpsimd.tensor_scalar(var_eps[:], mean_var[:, 1:2], EPS, None, ALU.add).then_inc(s["eps_added"], 1)
                    pool.wait_ge(s["eps_added"], n + 3)
                    nc.gpsimd.tensor_tensor(rstd[:], var_eps[:], half[:], ALU.pow).then_inc(s["rstd_ready"], 1)
                if there(n, c, -2):
                    pool.wait_ge(s["y_taken"], n - 1)
                    row = x[:, n - 2, :] if isinstance(n, int) else x[:, bass.ds(n - 2, 1), :]
                    y = y_sb[:] if isinstance(n, int) else y_sb[:].rearrange("p (o t) -> p o t", o=1)
                    nc.gpsimd.tensor_tensor(row, row, y, ALU.add).then_inc(s["y_free"], 1)
                for a in "kq":
                    if there(n, c, 2):
                        r, before = (c + 2) % RING, (c + 1) % RING
                        stacked = {"q": [q_stacked], "k": k_stacked}[a]
                        pool.wait_ge(s[a + "_roped"], n + 3)
                        nc.gpsimd.tensor_tensor(whole[a][:], roped[a][:, 0, :], roped[a][:, 1, :], ALU.add)\
                            .then_inc(s[a + "_summed"], 1)
                        pool.wait_ge(s[a + "_summed"], n + 3)
                        if there(n, c, 1):
                            for of_ring in stacked:
                                pool.wait_ge(of_ring[before], (48 if a == "q" else 96) * uses(c, i, 1))
                        wait_alone(pool)
                        nc.gpsimd.tensor_copy(part[a][:, 0, :], whole[a][:]).then_inc(s[a + "_high"], 1)
                        pool.wait_ge(s[a + "_high"], n + 3)
                        nc.gpsimd.tensor_tensor(part[a][:, 1, :], whole[a][:], part[a][:, 0, :].bitcast(F32),
                                                ALU.subtract).then_inc(s[a + "_split"], 1)

            steps(pool, body)

        @block.vector
        def _(dve):
            for r in range(RING):
                nc.vector.memset(v_st[r][:], 0.0).then_inc(s["values_cleared"], 1)
            for r in (0, 1):
                nc.vector.memset(k_st[r][0:ROWS, :, :, :].bitcast(F32), 0.0).then_inc(s["first_cleared"], 1)
            dve.wait_ge(s["values_cleared"], RING)
            for r in range(RING):
                nc.vector.memset(v_st[r][:, :, :, DH:DH + 1], 1.0).then_inc(s["ones_set"], 1)
            dve.wait_ge(s["ones_set"], RING)
            dve.wait_ge(consts_in, 6 * 16)
            nc.vector.tensor_tensor(out_bias[:], tanh_gain[:, 0:1], bias[:, 4:5], ALU.mult).then_inc(s["bias_ready"], 1)
            dve.wait_ge(x_first_in, 16)

            def rope_parts(a, n, c, cols):
                dve.wait_ge(s[a + "_projected"], n + 3)
                wait_count(dve, s[a + "_summed"], n + 2)
                for t in range(2):
                    last = nc.vector.scalar_tensor_tensor(
                        out=roped[a][:, t, :], in0=misc[:, t * D:(t + 1) * D], scalar=bias[:, cols + t:cols + t + 1],
                        in1=rope[:, t, :], op0=ALU.add, op1=ALU.mult)
                last.then_inc(s[a + "_roped"], 1)

            def body(n, c, i):
                for s_ in range(HP):
                    if s_ == 0 and there(n, c, 2):
                        row = x[:, n + 2, :] if isinstance(n, int) else x[:, bass.ds(n + 2, 1), :]
                        wait_count(dve, s["stats_done"], n + 2)
                        nc.vector.bn_stats(stats[:], row).then_inc(s["stats_raw"], 1)
                        dve.wait_ge(s["stats_raw"], n + 3)
                        wait_count(dve, s["xn_ready"], n + 2)
                        wait_count(dve, s["eps_added"], n + 2)
                        wait_alone(dve)
                        nc.vector.bn_aggr(mean_var[:], stats[:]).then_inc(s["stats_done"], 1)
                    if s_ == 0:
                        if there(n, c, 0):
                            dve.wait_ge(s["max_taken"], (n + 1) * (HP // 2))
                            wait_count(dve, s["m_turned"], n)
                            nc.vector.tensor_scalar(m_parts[:, 0:2 * HP].bitcast(F32R), row_max[c % 2][:], -1.0, None,
                                                    ALU.mult).then_inc(s["m_high"], 1)
                            dve.wait_ge(s["m_high"], n + 1)
                            nc.vector.scalar_tensor_tensor(out=m_parts[:, 2 * HP:4 * HP].bitcast(F32R),
                                                           in0=row_max[c % 2][:], scalar=-1.0,
                                                           in1=m_parts[:, 0:2 * HP], op0=ALU.mult,
                                                           op1=ALU.subtract).then_inc(s["m_split"], 1)
                    if s_ == 2 and there(n, c, 0):
                        dve.wait_ge(s["m_turned"], n + 1)
                        if there(n, c, -1):
                            dve.wait_ge(m_stacked[(c - 1) % RING], 16 * uses(c, i, -1))
                        nc.vector.tensor_copy(m_rows[:], misc[0:4 * HP, 0:P]).then_inc(s["m_taken"], 1)
                    if s_ == 2 and there(n, c, 2):
                        row = x[:, n + 2, :] if isinstance(n, int) else x[:, bass.ds(n + 2, 1), :]
                        out = xn[:] if isinstance(n, int) else xn[:].rearrange("p (o t) -> p o t", o=1)
                        dve.wait_ge(s["rstd_ready"], n + 3)
                        dve.wait_ge(s["stats_done"], n + 3)
                        wait_count(dve, s["q_projected"], n + 2)
                        nc.vector.tensor_scalar(out, row, mean_var[:, 0:1], rstd[:], ALU.subtract, ALU.mult)\
                            .then_inc(s["xn_ready"], 1)
                    if s_ == 4 and there(n, c, 2):
                        rope_parts("k", n, c, 2)
                    if s_ == 6 and there(n, c, 2):
                        rope_parts("q", n, c, 0)
                    if s_ == 8 and there(n, c, 2):
                        r = (c + 2) % RING
                        dve.wait_ge(s["v_projected"], n + 3)
                        wait_count(dve, s["pv_done"], UNITS * (n - 1))
                        for h in range(2):
                            last = nc.vector.tensor_tensor(
                                v_st[r][:, h, :, 0:DH], misc[:, h * P:(h + 1) * P].rearrange("p (h d) -> p h d", d=DH),
                                bias_v[:].rearrange("p (h d) -> p h d", d=DH), ALU.add)
                        last.then_inc(s["v_stored"], 1)
                    if s_ in (10, 12) and there(n, c, -1):
                        b = s_ // 12
                        o = misc[:, :].rearrange("p (h r) -> p h r", r=32)
                        k = 2 * (n - 1) + b
                        dve.wait_ge(s["o_turned"], k + 1)
                        nc.vector.reciprocal(o_rcp[:].unsqueeze(2), o[:, :, DH:DH + 1]).then_inc(s["rcp_ready"], 1)
                        dve.wait_ge(s["rcp_ready"], k + 1)
                        if b == 0:
                            wait_count(dve, s["a_turned"], n - 1)
                        nc.vector.tensor_tensor(
                            a_sb[:, :, b, :].rearrange("p h (j d) -> p h j d", d=DH),
                            o[:, :, 0:DH].rearrange("p (h j) d -> p h j d", h=2),
                            o_rcp[:].rearrange("p (h j) -> p h j", h=2).unsqueeze(3).to_broadcast([P, 2, HEADS, DH]),
                            ALU.mult).then_inc(s["o_normed"], 1)
                    if s_ % 2 == 0 and there(n, c, 1):
                        g = (n + 1) * (HP // 2) + s_ // 2
                        dve.wait_ge(s["scored"], g + 1)
                        if s_ == 0:
                            wait_count(dve, s["m_split"], n)
                        u, j = s_ // UH, s_ % UH
                        out = row_max[(c + 1) % 2][:].rearrange("p (j u h) -> p j u h", j=UH, u=UNITS)[:, j:j + 2, u, :]
                        nc.vector.tensor_reduce(out, s_ps[s_ // 2 % 2][:].rearrange("p (j h) t -> p j h t", j=2),
                                                AX_X, ALU.max).then_inc(s["max_taken"], 1)

            steps(dve, body, lambda: dve.wait_ge(x_rest_in, 32))

        @block.scalar
        def _(act):
            act.wait_ge(consts_in, 6 * 16)
            for r in range(RING):
                nc.scalar.copy(k_st[r][ROWS:MROWS, :, :, :],
                               own_head[ROWS:MROWS, :].unsqueeze(1).unsqueeze(3)
                               .to_broadcast([MROWS - ROWS, UNITS, UH, D])).then_inc(s["own_set"], 1)
            act.wait_ge(s["bias_ready"], 1)

            def body(n, c, i):
                for s_ in range(HP):
                    if s_ == 14 and there(n, c, -1):
                        act.wait_ge(s["a_turned"], n)
                        wait_count(act, s["y_projected"], n - 1)
                        nc.scalar.copy(a_t[:], misc[:, 0:D]).then_inc(s["a_taken"], 1)
                    if s_ == 0 and there(n, c, -2):
                        act.wait_ge(s["y_projected"], n - 1)
                        act.wait_ge(s["y_free"], n - 1)
                        nc.scalar.activation(y_sb[:], misc[:, 0:D], ACT.Identity, bias=out_bias[:],
                                             scale=tanh_gain[:, 0:1]).then_inc(s["y_taken"], 1)
                    k, h = st_head(s_)
                    if there(n, c, k):
                        g = HP * (n + k) + h
                        act.wait_ge(s["st_scored"], g + 1)
                        if h % UH == 0:
                            wait_count(act, s["pv_done"], UNITS * (n + k) + h // UH - 1)
                        nc.scalar.activation(e_t[h % 8][:], st_ps[h % 2][:], ACT.Exp, scale=float(DH) ** -0.5)\
                            .then_inc(s["exp_done"], 1)
                    if s_ in (2, 10) and there(n, c, -1):
                        b = s_ // 10
                        act.wait_ge(s["pv_done"], UNITS * (n - 1) + 2 * b + 2)
                        wait_count(act, s["o_turned"], 2 * (n - 1) + b - 1)
                        nc.scalar.copy(o_sb[b][:], o_ps[:]).then_inc(s["o_taken"], 1)

            steps(act, body)

        @block.tensor
        def _(pe):
            pe.wait_ge(consts_in, 6 * 16)

            def project(a, n, c, at, rhs):
                for t in range(2):
                    last = nc.tensor.matmul(misc[:, t * D:(t + 1) * D], w_in[:, at + t, :], rhs,
                                            start=True, stop=True)
                last.then_inc(s[a + "_projected"], 1)

            def body(n, c, i):
                for s_ in range(HP):
                    if s_ == 0 and there(n, c, -2):
                        pe.wait_ge(s["a_taken"], n - 1)
                        nc.tensor.matmul(misc[:, 0:D], w_out[:], a_t[:], start=True, stop=True)\
                            .then_inc(s["y_projected"], 1)
                    if s_ == 2 and there(n, c, 0):
                        wait_count(pe, s["v_stored"], min(n, 1) + 2 if isinstance(n, int) else 0)
                        wait_count(pe, s["y_taken"], n - 1)
                        pe.wait_ge(s["m_split"], n + 1)
                        wait_alone(pe)
                        nc.tensor.transpose(misc[0:4 * HP, 0:P], m_parts[:], ident[:]).then_inc(s["m_turned"], 1)
                    if s_ == 4 and there(n, c, 2):
                        wait_count(pe, s["m_taken"], n + 1)
                        if isinstance(n, int):
                            wait_count(pe, s["v_stored"], n + 2)
                        pe.wait_ge(c_loaded[(c + 2) % RING], 16 * uses(c, i, 2))
                        project("k", n, c, 2, c_in[(c + 2) % RING][:])
                    if s_ == 6 and there(n, c, 2):
                        pe.wait_ge(s["k_roped"], n + 3)
                        pe.wait_ge(s["xn_ready"], n + 3)
                        project("q", n, c, 0, xn[:])
                    if s_ == 8 and there(n, c, 2):
                        pe.wait_ge(s["q_roped"], n + 3)
                        for h in range(2):
                            last = nc.tensor.matmul(misc[:, h * P:(h + 1) * P],
                                                    c_in[(c + 2) % RING][:, h * P:(h + 1) * P], w_in[:, 4, :],
                                                    start=True, stop=True)
                        last.then_inc(s["v_projected"], 1)
                    if s_ in (10, 12) and there(n, c, -1):
                        b = s_ // 12
                        if b == 1:
                            pe.wait_ge(s["o_normed"], 2 * (n - 1) + 1)
                        elif there(n, c, 2):
                            pe.wait_ge(s["v_stored"], n + 3)
                        elif there(n, c, 0):
                            pe.wait_ge(s["m_taken"], n + 1)
                        else:
                            pe.wait_ge(s["y_taken"], n - 1)
                        pe.wait_ge(s["o_taken"], 2 * (n - 1) + b + 1)
                        for half_, u in ((h, u) for h in range(2) for u in range(2)):
                            at = (2 * half_ + u) * P
                            last = nc.tensor.transpose(misc[:, at:at + P], o_sb[b][:, u, half_ * P:(half_ + 1) * P],
                                                       ident[:])
                        last.then_inc(s["o_turned"], 1)
                    if s_ == 14 and there(n, c, -1):
                        pe.wait_ge(s["o_normed"], 2 * n)
                        for h in range(2):
                            last = nc.tensor.transpose(misc[:, h * P:(h + 1) * P], a_sb[:, h, :, :], ident[:])
                        last.then_inc(s["a_turned"], 1)

                    if s_ % 2 == 0 and there(n, c, 1):
                        r = (c + 1) % RING
                        g = (n + 1) * (HP // 2) + s_ // 2
                        if s_ == 0:
                            pe.wait_ge(q_stacked[r], 48 * uses(c, i, 1))
                        if s_ in (0, 2):
                            pe.wait_ge(k_stacked[s_ // 2][r], 96 * uses(c, i, 1))
                        wait_count(pe, s["max_taken"], g - 1)
                        for h in (s_, s_ + 1):
                            u, j = h // UH, h % UH
                            for half_ in range(2):
                                last = nc.tensor.matmul(s_ps[s_ // 2 % 2][:, 2 * (h - s_) + half_, :],
                                                        q_st[r][0:ROWS, u, half_ * P:(half_ + 1) * P],
                                                        k_st[r][0:ROWS, u, j, :], start=True, stop=True)
                        last.then_inc(s["scored"], 1)

                    k, h = st_head(s_)
                    if there(n, c, k):
                        r = (c + k) % RING
                        g = HP * (n + k) + h
                        if h == 0:
                            pe.wait_ge(m_stacked[r], 16 * uses(c, i, k))
                            if isinstance(n, int) and n == 0:
                                pe.wait_ge(s["own_set"], RING)
                        wait_count(pe, s["exp_done"], g - 1)
                        u, j = h // UH, h % UH
                        for half_ in range(2):
                            last = nc.tensor.matmul(st_ps[h % 2][:, half_, :],
                                                    k_st[r][0:MROWS, u, j, half_ * P:(half_ + 1) * P],
                                                    q_st[r][0:MROWS, u, :], start=True, stop=True)
                        last.then_inc(s["st_scored"], 1)

                    k, h = st_head((s_ - 2) % HP)
                    if s_ < 2:
                        k -= 1 if (s_ - 2) % HP >= LAG else 0
                    if h % UH == UH - 1 and there(n, c, k):
                        r = (c + k) % RING
                        u = h // UH
                        pe.wait_ge(s["exp_done"], HP * (n + k) + h + 1)
                        if u == 0:
                            pe.wait_ge(s["v_stored"], n + k + 1)
                        if u % 2 == 0:
                            wait_count(pe, s["o_taken"], 2 * (n + k) + u // 2)
                        for half_ in range(2):
                            for j in range(UH):
                                last = nc.tensor.matmul(o_ps[32 * j:32 * j + 32, u % 2, :],
                                                        v_st[r][:, half_, u * UH + j, :],
                                                        e_t[(u * UH + j) % 8][:, half_, :],
                                                        start=(half_ == 0), stop=(half_ == 1))
                        last.then_inc(s["pv_done"], 1)

            steps(pe, body)


def feed_forward(nc, dram, x, ident, tanh_gain, gain_at, hidden, passes, weights, routed, out=None):
    CHUNKS = hidden // P
    PIECE = 2 * hidden
    RINGS = 2 if passes > 1 else 1
    ROUTER = 8

    with ExitStack() as ctx:
        def sb(name, shape, dt=F32):
            return ctx.enter_context(nc.sbuf_tensor(name + tag, shape, dt))

        def ps(name, shape, dt=F32):
            return ctx.enter_context(nc.psum_tensor(name + tag, shape, dt))

        def sem(name):
            return nc.alloc_semaphore(name + tag)

        tag = "_moe" if routed else "_ffn"
        xt_hi = sb("xt_hi", [P, 2, BATCH * CH], F32R)
        xt_lo = sb("xt_lo", [P, 2, BATCH * CH], F32R)
        xn = sb("xn", [P, GT, D])
        stats = sb("stats", [P, GT, 6])
        mean_var = sb("mean_var", [P, GT, 2])
        var_eps = sb("var_eps", [P, GT])
        rstd = sb("rstd", [P, GT])
        half = sb("half", [P, GT])
        stage = [sb(f"stage{r}", [P, PIECE]) for r in range(2)]
        w_hi = [sb(f"w_hi{r}", [P, 3, PIECE], F32R) for r in range(RINGS)]
        w_lo = [sb(f"w_lo{r}", [P, 3, PIECE], F32R) for r in range(RINGS)]
        silu = [sb(f"silu{r}", [P, GROUP]) for r in range(2)]
        h_all = [sb(f"h_all{r}", [P, GROUP]) for r in range(2)]
        h_hi = sb("h_hi", [P, CHUNKS, GROUP], F32R)
        h_lo = sb("h_lo", [P, CHUNKS, GROUP], F32R)
        combine = sb("combine", [P, passes, TILES])
        now = sb("now", [P, GT])

        g_ps = [ps(f"g_ps{r}", [P, GROUP]) for r in range(2)]
        u_ps = [ps(f"u_ps{r}", [P, GROUP]) for r in range(2)]
        y_ps = ps("y_ps", [P, GT, D])
        t_ps = [ps(f"t_ps{r}", [P, GROUP]) for r in range(2)]

        piece_in = [sem(f"piece_in{r}") for r in range(2)]
        out_stored = sem("out_stored")
        names = ("stats_raw stats_done eps_added rstd_ready xn_ready half_set first_high first_split turned hi_taken lo_taken w_high w_split "
                 "gate_done up_done silu_done product_done hi_done lo_done down_done shared_set now_set "
                 "added").split()
        s = {name: sem(name) for name in names}
        if routed:
            router_in = sem("router_in")
            router_w = sb("router_w", [P, 2, ROUTER])
            router_hi = sb("router_hi", [P, 2, ROUTER], F32R)
            router_lo = sb("router_lo", [P, 2, ROUTER], F32R)
            earlier = sb("earlier", [P, ROUTER, ROUTER])
            logits_t = sb("logits_t", [ROUTER, GROUP])
            logits = sb("logits", [P, GT, ROUTER])
            above = sb("above", [P, GT, ROUTER, ROUTER])
            level = sb("level", [P, GT, ROUTER, ROUTER])
            rank = sb("rank", [P, GT, ROUTER])
            chosen = sb("chosen", [P, GT, ROUTER])
            chosen_logits = sb("chosen_logits", [P, GT, ROUTER])
            pair_sum = sb("pair_sum", [P, GT])
            lead = sb("lead", [P, GT, ROUTER])
            tanh_lead = sb("tanh_lead", [P, GT, ROUTER])
            share = sb("share", [P, GT, ROUTER])
            rs = {name: sem(name) for name in ("router_high router_split logits_made logits_taken logits_turned "
                                               "logits_ready levels_made levels_less levels_masked above_added "
                                               "ranked chosen_set chosen_made sum_made lead_ready tanh_made "
                                               "share_made routed_done").split()}

        def all_steps(eng, body):
            body(0, 0, 0, True, True)
            with eng.Fori(1, GROUPS - 1) as g:
                body(0, 0, g, True, True)
            body(0, 0, GROUPS - 1, True, False)
            if passes > 1:
                with eng.Fori(0, (passes - 1) // 2) as i:
                    for t in range(2):
                        with eng.Fori(0, GROUPS) as g:
                            body(2 * i + 1 + t, (1 + t) % 2, g, False, False)

        def tile(g, t):
            return x[:, GT * g + t, :] if isinstance(g, int) else x[:, bass.ds(GT * g + t, 1), :]

        def flat(ap, g):
            return ap if isinstance(g, int) else ap.unsqueeze(1)

        def cols(buffer, kc, g):
            return buffer[:, kc, g * GROUP:(g + 1) * GROUP] if isinstance(g, int) \
                else buffer[:, kc, bass.ds(g * GROUP, GROUP)]

        block = ctx.enter_context(nc.Block())

        @block.sync
        def _(sp):
            if routed:
                sp.dma_start(router_w[:], dram["router"]).then_inc(router_in, 16)
                sp.dma_start(earlier[:], dram["earlier"]).then_inc(router_in, 16)

            def load(i, c, src):
                sp.wait_ge(s["w_split"], 6 * i + c - 1)
                sp.dma_start(stage[c % 2][:], src).then_inc(piece_in[c % 2], 16)

            for c in range(3):
                if c == 2:
                    sp.wait_ge(s["first_split"], 1)
                sp.dma_start(stage[c % 2][:], weights[c] if passes == 1 else weights[0, c])\
                    .then_inc(piece_in[c % 2], 16)
            if passes > 1:
                with sp.Fori(0, (passes - 1) // 2) as i:
                    for c in range(3, 9):
                        load(i, c, weights[bass.ds(2 * i + c // 3, 1), c % 3, :, :])
            if out is not None:
                rows = out.rearrange("(n b) c t -> (b c) n t", b=2)
                with sp.Fori(0, GROUPS) as g:
                    sp.wait_ge(s["added"], g + 1)
                    sp.dma_start(rows[:, bass.ds(GT * g, GT), :], x[:, bass.ds(GT * g, GT), :]).then_inc(out_stored, 16)
                sp.wait_ge(out_stored, 16 * GROUPS)

        @block.gpsimd
        def _(pool):
            nc.gpsimd.memset(half[:], -0.5).then_inc(s["half_set"], 1)
            pool.wait_ge(s["half_set"], 1)

            def rstd_of(g):
                pool.wait_ge(s["stats_done"], g + 1)
                wait_count(pool, s["xn_ready"], g)
                wait_alone(pool)
                nc.gpsimd.tensor_scalar(var_eps[:].unsqueeze(2), mean_var[:, :, 1:2], EPS, None, ALU.add)\
                    .then_inc(s["eps_added"], 1)
                pool.wait_ge(s["eps_added"], g + 1)
                nc.gpsimd.tensor_tensor(rstd[:], var_eps[:], half[:], ALU.pow).then_inc(s["rstd_ready"], 1)

            def split(i, c):
                k, ring, of = 2 * i + c // 3, c // 3 % RINGS, c % 3
                pool.wait_ge(piece_in[c % 2], 16 * (3 * i + c // 2 + 1))
                pool.wait_ge(s["down_done"], CHUNKS * GROUPS * (k - 1) + 1)
                wait_alone(pool)
                nc.gpsimd.tensor_copy(w_hi[ring][:, of, :], stage[c % 2][:]).then_inc(s["w_high"], 1)
                pool.wait_ge(s["w_high"], 6 * i + c - 2)
                nc.gpsimd.tensor_tensor(w_lo[ring][:, of, :], stage[c % 2][:], w_hi[ring][:, of, :].bitcast(F32),
                                        ALU.subtract).then_inc(s["w_split"], 1)

            rstd_of(0)
            for g in range(1, GROUPS):
                rstd_of(g)
            if passes > 1:
                with pool.Fori(0, (passes - 1) // 2) as i:
                    for c in range(3, 9):
                        split(i, c)

        @block.scalar
        def _(act):
            def high_of(g):
                for kc in range(2):
                    act.wait_ge(s["turned"], 2 * g + kc + 1)
                    nc.scalar.copy(cols(xt_hi, kc, g), t_ps[kc][:]).then_inc(s["hi_taken"], 1)

            def body(k, r, g, shared, ahead):
                q = GROUPS * k + g

                def high(m):
                    n = CHUNKS * q + m
                    act.wait_ge(s["product_done"], n + 1)
                    wait_count(act, s["down_done"], n + 1 - CHUNKS)
                    nc.scalar.copy(h_hi[:, m, :], h_all[m % 2][:]).then_inc(s["hi_done"], 1)

                for m in range(CHUNKS):
                    n = CHUNKS * q + m
                    act.wait_ge(s["gate_done"], n + 1)
                    wait_count(act, s["product_done"], n - 1)
                    nc.scalar.activation(silu[m % 2][:], g_ps[m % 2][:], ACT.Silu).then_inc(s["silu_done"], 1)
                    if m == 0 and shared and routed:
                        act.wait_ge(rs["logits_made"], g + 1)
                        wait_count(act, rs["logits_turned"], g)
                        nc.scalar.copy(logits_t[:], t_ps[0][0:ROUTER, :]).then_inc(rs["logits_taken"], 1)
                    if m > 0:
                        high(m - 1)
                high(CHUNKS - 1)
                if ahead:
                    high_of(g + 1)
                if shared and routed:
                    act.wait_ge(rs["lead_ready"], g + 1)
                    nc.scalar.activation(tanh_lead[:], lead[:], ACT.Tanh).then_inc(rs["tanh_made"], 1)

            for c in range(3):
                act.wait_ge(piece_in[c % 2], 16 * (c // 2 + 1))
                nc.scalar.copy(w_hi[0][:, c, :], stage[c % 2][:]).then_inc(s["first_high"], 1)
                if c == 0:
                    high_of(0)
            all_steps(act, body)

        @block.vector
        def _(dve):
            def stats_of(g):
                for t in range(GT):
                    last = nc.vector.bn_stats(stats[:, t, :], tile(g, t))
                last.then_inc(s["stats_raw"], 1)
                dve.wait_ge(s["stats_raw"], g + 1)
                wait_count(dve, s["eps_added"], g)
                wait_count(dve, s["xn_ready"], g)
                wait_alone(dve)
                for t in range(GT):
                    last = nc.vector.bn_aggr(mean_var[:, t, :], stats[:, t, :])
                last.then_inc(s["stats_done"], 1)

            def norm_of(g):
                dve.wait_ge(s["rstd_ready"], g + 1)
                wait_count(dve, s["turned"], 2 * g)
                for t in range(GT):
                    last = nc.vector.tensor_scalar(flat(xn[:, t, :], g), tile(g, t), mean_var[:, t, 0:1],
                                                   rstd[:, t:t + 1], ALU.subtract, ALU.mult)
                last.then_inc(s["xn_ready"], 1)

            def low_of(g):
                for kc in range(2):
                    dve.wait_ge(s["hi_taken"], 2 * g + kc + 1)
                    nc.vector.tensor_tensor(cols(xt_lo, kc, g), t_ps[kc][:], cols(xt_hi, kc, g).bitcast(F32),
                                            ALU.subtract).then_inc(s["lo_taken"], 1)

            if routed:
                dve.wait_ge(router_in, 32)
                nc.vector.tensor_copy(router_hi[:], router_w[:]).then_inc(rs["router_high"], 1)
                dve.wait_ge(rs["router_high"], 1)
                nc.vector.tensor_tensor(router_lo[:], router_w[:], router_hi[:].bitcast(F32), ALU.subtract)\
                    .then_inc(rs["router_split"], 1)
            nc.vector.tensor_copy(combine[:, 0, :], tanh_gain[:, gain_at:gain_at + 1].to_broadcast([P, TILES]))\
                .then_inc(s["shared_set"], 1)
            dve.wait_ge(s["shared_set"], 1)

            def route(g):
                one, two = logits[:].unsqueeze(3), logits[:].unsqueeze(2)
                wide = [P, GT, ROUTER, ROUTER]
                nc.vector.tensor_tensor(above[:], two.to_broadcast(wide), one.to_broadcast(wide), ALU.is_gt)
                nc.vector.tensor_tensor(level[:], two.to_broadcast(wide), one.to_broadcast(wide), ALU.is_ge)\
                    .then_inc(rs["levels_made"], 1)
                dve.wait_ge(rs["levels_made"], g + 1)
                nc.vector.tensor_tensor(level[:], level[:], above[:], ALU.subtract).then_inc(rs["levels_less"], 1)
                dve.wait_ge(rs["levels_less"], g + 1)
                nc.vector.tensor_tensor(level[:].rearrange("p t a b -> p t (a b)"),
                                        level[:].rearrange("p t a b -> p t (a b)"),
                                        earlier[:].rearrange("p a b -> p (a b)").unsqueeze(1)
                                        .to_broadcast([P, GT, ROUTER * ROUTER]), ALU.mult)\
                    .then_inc(rs["levels_masked"], 1)
                dve.wait_ge(rs["levels_masked"], g + 1)
                nc.vector.tensor_tensor(above[:], above[:], level[:], ALU.add).then_inc(rs["above_added"], 1)
                dve.wait_ge(rs["above_added"], g + 1)
                nc.vector.tensor_reduce(rank[:], above[:], AX_X, ALU.add).then_inc(rs["ranked"], 1)
                dve.wait_ge(rs["ranked"], g + 1)
                nc.vector.tensor_scalar(chosen[:], rank[:], 2.0, None, ALU.is_lt).then_inc(rs["chosen_set"], 1)
                dve.wait_ge(rs["chosen_set"], g + 1)
                nc.vector.tensor_tensor(chosen_logits[:], chosen[:], logits[:], ALU.mult).then_inc(rs["chosen_made"], 1)
                dve.wait_ge(rs["chosen_made"], g + 1)
                nc.vector.tensor_reduce(pair_sum[:], chosen_logits[:], AX_X, ALU.add).then_inc(rs["sum_made"], 1)
                dve.wait_ge(rs["sum_made"], g + 1)
                nc.vector.scalar_tensor_tensor(out=lead[:], in0=pair_sum[:].unsqueeze(2).to_broadcast([P, GT, ROUTER]),
                                               scalar=-0.5, in1=logits[:], op0=ALU.mult, op1=ALU.add)\
                    .then_inc(rs["lead_ready"], 1)
                dve.wait_ge(rs["tanh_made"], g + 1)
                nc.vector.scalar_tensor_tensor(out=share[:], in0=tanh_lead[:], scalar=1.0, in1=chosen[:],
                                               op0=ALU.add, op1=ALU.mult).then_inc(rs["share_made"], 1)
                dve.wait_ge(rs["share_made"], g + 1)
                for t in range(GT):
                    at = GT * g + t
                    dst = combine[:, 1:passes, at:at + 1] if isinstance(g, int) else combine[:, 1:passes, bass.ds(at, 1)]
                    last = nc.vector.tensor_scalar(dst, share[:, t, :].unsqueeze(2), tanh_gain[:, gain_at:gain_at + 1],
                                                   0.5, ALU.mult, ALU.mult)
                last.then_inc(rs["routed_done"], 1)

            def body(k, r, g, shared, ahead):
                q = GROUPS * k + g

                def low(m):
                    n = CHUNKS * q + m
                    dve.wait_ge(s["hi_done"], n + 1)
                    wait_count(dve, s["down_done"], n + 1 - CHUNKS)
                    nc.vector.tensor_tensor(h_lo[:, m, :], h_all[m % 2][:], h_hi[:, m, :].bitcast(F32), ALU.subtract)\
                        .then_inc(s["lo_done"], 1)

                if routed and not shared:
                    dve.wait_ge(rs["routed_done"], GROUPS)
                weight = combine[:, k, GT * g:GT * g + GT] if isinstance(g, int) and isinstance(k, int) else \
                    combine[:].rearrange("p k t -> p (k t)")[:, bass.ds(k * TILES + GT * g, GT)]
                wait_count(dve, s["added"], q)
                nc.vector.tensor_copy(now[:], weight).then_inc(s["now_set"], 1)
                for m in range(CHUNKS):
                    n = CHUNKS * q + m
                    dve.wait_ge(s["silu_done"], n + 1)
                    dve.wait_ge(s["up_done"], n + 1)
                    wait_count(dve, s["lo_done"], n - 1)
                    nc.vector.tensor_tensor(h_all[m % 2][:], silu[m % 2][:], u_ps[m % 2][:], ALU.mult)\
                        .then_inc(s["product_done"], 1)
                    if m == 0 and ahead:
                        stats_of(g + 1)
                    if m > 0:
                        low(m - 1)
                    if m == 1 and ahead:
                        norm_of(g + 1)
                    if m == 2 and shared and routed:
                        dve.wait_ge(rs["logits_turned"], g + 1)
                        nc.vector.tensor_copy(logits[:].rearrange("p t e -> p (t e)"), t_ps[1][:, 0:GT * ROUTER])\
                            .then_inc(rs["logits_ready"], 1)
                low(CHUNKS - 1)
                if ahead:
                    low_of(g + 1)
                if shared and routed:
                    dve.wait_ge(rs["logits_ready"], g + 1)
                    route(g)
                dve.wait_ge(s["down_done"], CHUNKS * (q + 1))
                dve.wait_ge(s["now_set"], q + 1)
                for t in range(GT):
                    y = flat(y_ps[:, t, :], g)
                    last = nc.vector.scalar_tensor_tensor(out=tile(g, t), in0=y, scalar=now[:, t:t + 1],
                                                          in1=tile(g, t), op0=ALU.mult, op1=ALU.add)
                last.then_inc(s["added"], 1)

            stats_of(0)
            norm_of(0)
            for c in range(3):
                dve.wait_ge(s["first_high"], c + 1)
                low = nc.vector.tensor_tensor(w_lo[0][:, c, :], stage[c % 2][:], w_hi[0][:, c, :].bitcast(F32),
                                              ALU.subtract)
                if c == 0:
                    low.then_inc(s["first_split"], 1)
                    low_of(0)
                elif c == 2:
                    low.then_inc(s["w_split"], 3)
            all_steps(dve, body)

        @block.tensor
        def _(pe):
            def turn(g):
                pe.wait_ge(s["xn_ready"], g + 1)
                wait_count(pe, s["lo_taken"], 2 * g)
                if routed:
                    wait_count(pe, rs["logits_ready"], g)
                for kc in range(2):
                    for t in range(GT):
                        last = nc.tensor.transpose(t_ps[kc][:, t * P:(t + 1) * P], xn[:, t, kc * P:(kc + 1) * P], ident[:])
                    last.then_inc(s["turned"], 1)

            def body(k, r, g, shared, ahead):
                q = GROUPS * k + g

                def products(m):
                    n = CHUNKS * q + m
                    for bank, base, before, done in ((g_ps, 0, "silu_done", "gate_done"),
                                                     (u_ps, hidden, "product_done", "up_done")):
                        wait_count(pe, s[before], n - 1)
                        at = base + m * P
                        terms = [(w, xt, kc) for kc in range(2) for w, xt in
                                 ((w_hi[r], xt_hi), (w_lo[r], xt_hi), (w_hi[r], xt_lo))]
                        for t, (w, xt, kc) in enumerate(terms):
                            last = nc.tensor.matmul(bank[m % 2][:], w[:, kc, at:at + P], cols(xt, kc, g),
                                                    start=(t == 0), stop=(t == 5))
                        last.then_inc(s[done], 1)

                def down(m):
                    pe.wait_ge(s["lo_done"], CHUNKS * q + m + 1)
                    if m == 0:
                        wait_count(pe, s["added"], q)
                    for t in range(GT):
                        for a, (h, w) in enumerate(((h_hi, w_hi[r]), (h_hi, w_lo[r]), (h_lo, w_hi[r]))):
                            last = nc.tensor.matmul(y_ps[:, t, :], h[:, m, t * P:(t + 1) * P],
                                                    w[:, 2, m * D:(m + 1) * D],
                                                    start=(m == 0 and a == 0 and t % 2 == 0),
                                                    stop=(m == CHUNKS - 1 and a == 2), skip_group_check=True)
                    last.then_inc(s["down_done"], 1)

                pe.wait_ge(s["w_split"], 3 * (k + 1))
                for m in range(CHUNKS):
                    products(m)
                    if m == 0 and shared and routed:
                        for t, (w, xt, kc) in enumerate([(w, xt, kc) for kc in range(2) for w, xt in
                                                         ((router_hi, xt_hi), (router_lo, xt_hi), (router_hi, xt_lo))]):
                            last = nc.tensor.matmul(t_ps[0][0:ROUTER, :], w[:, kc, :], cols(xt, kc, g),
                                                    start=(t == 0), stop=(t == 5))
                        last.then_inc(rs["logits_made"], 1)
                    if m == 1 and shared and routed:
                        pe.wait_ge(rs["logits_taken"], g + 1)
                        wait_alone(pe)
                        for t in range(GT):
                            last = nc.tensor.transpose(t_ps[1][:, t * ROUTER:(t + 1) * ROUTER],
                                                       logits_t[:, t * P:(t + 1) * P], ident[0:ROUTER, 0:ROUTER])
                        last.then_inc(rs["logits_turned"], 1)
                    if m == CHUNKS - 1 and ahead:
                        turn(g + 1)
                    if m >= 2:
                        down(m - 2)
                down(CHUNKS - 2)
                down(CHUNKS - 1)

            turn(0)
            if routed:
                pe.wait_ge(rs["router_split"], 1)
            pe.wait_ge(s["lo_taken"], 2)

            def stepped(k, r, g, shared, ahead):
                if shared:
                    pe.wait_ge(s["lo_taken"], 2 * g + 2)
                body(k, r, g, shared, ahead)

            all_steps(pe, stepped)


def pooled_context(nc, dram, ident, pooled, decay):
    RH = 8
    with ExitStack() as ctx:
        def sb(name, shape, dt=F32):
            return ctx.enter_context(nc.sbuf_tensor(name, shape, dt))

        def ps(name, shape, dt=F32):
            return ctx.enter_context(nc.psum_tensor(name, shape, dt))

        def sem(name):
            return nc.alloc_semaphore(name)

        c_all = sb("c_all", [P, TILES, D])
        batch_ones = sb("batch_ones", [P, 2])
        sums = sb("sums", [P, TILES * RH])
        row_max = sb("pool_max", [P, 2, 2])
        shifted = sb("shifted", [P, 2, 2, CH])
        exps = sb("exps", [P, 2, 2, CH])
        total = sb("total", [P, 2, 2])
        attn_t = sb("attn_t", [P, 2, 2, CH])
        attn = sb("attn", [P, TILES * RH])
        a_param = sb("a_param", [P, 2])
        positive, magnitude, u, one_more, less, none, logged, ratio, result = \
            (sb("softplus_" + name, [P, 2]) for name in
             "positive magnitude u one_more less none logged ratio result".split())
        t_ps = [ps(f"pool_ps{r}", [P, P]) for r in range(2)]
        hp_ps = ps("hp_ps", [P, 2, BATCH])
        c_all_in = [sem(f"c_all_in{r}") for r in range(4)]
        small_in = sem("small_in")
        s = {name: sem("pool_" + name) for name in
             "summed turned maxed shifted_done exp_done totalled inverted attn_done turned_back attn_taken weighted "
             "pooled_done taken softplus_step".split()}
        block = ctx.enter_context(nc.Block())
        QUARTER = TILES // 4

        @block.sync
        def _(sp):
            rows = dram["ctx_2048"].rearrange("(n b) c t -> (b c) n t", b=2)
            sp.dma_start(batch_ones[:], dram["batch_ones"]).then_inc(small_in, 16)
            sp.dma_start(a_param[:], dram["a_param"]).then_inc(small_in, 16)
            for r in range(4):
                sp.dma_start(c_all[:, r * QUARTER:(r + 1) * QUARTER, :], rows[:, r * QUARTER:(r + 1) * QUARTER, :])\
                    .then_inc(c_all_in[r], 16)

        @block.vector
        def _(dve):
            dve.wait_ge(small_in, 32)
            nc.vector.tensor_scalar(positive[:], a_param[:], 0.0, None, ALU.max).then_inc(s["softplus_step"], 1)
            dve.wait_ge(s["softplus_step"], 1)
            nc.vector.scalar_tensor_tensor(out=magnitude[:], in0=a_param[:], scalar=-1.0, in1=a_param[:],
                                           op0=ALU.mult, op1=ALU.max).then_inc(s["softplus_step"], 1)
            dve.wait_ge(s["softplus_step"], 3)
            nc.vector.tensor_scalar(one_more[:], u[:], 1.0, None, ALU.add).then_inc(s["softplus_step"], 1)
            dve.wait_ge(s["softplus_step"], 4)
            nc.vector.tensor_scalar(less[:], one_more[:], -1.0, None, ALU.add).then_inc(s["softplus_step"], 1)
            dve.wait_ge(s["softplus_step"], 5)
            nc.vector.tensor_scalar(none[:], less[:], 0.0, None, ALU.is_equal).then_inc(s["softplus_step"], 1)
            dve.wait_ge(s["softplus_step"], 7)
            nc.vector.tensor_tensor(less[:], less[:], none[:], ALU.add).then_inc(s["softplus_step"], 1)
            dve.wait_ge(s["softplus_step"], 8)
            nc.vector.reciprocal(ratio[:], less[:]).then_inc(s["softplus_step"], 1)
            dve.wait_ge(s["softplus_step"], 9)
            nc.vector.tensor_tensor(ratio[:], ratio[:], u[:], ALU.mult).then_inc(s["softplus_step"], 1)
            dve.wait_ge(s["softplus_step"], 10)
            nc.vector.tensor_tensor(ratio[:], ratio[:], logged[:], ALU.mult).then_inc(s["softplus_step"], 1)
            dve.wait_ge(s["softplus_step"], 11)
            nc.vector.tensor_tensor(result[:], none[:], u[:], ALU.mult).then_inc(s["softplus_step"], 1)
            dve.wait_ge(s["softplus_step"], 12)
            nc.vector.tensor_tensor(ratio[:], ratio[:], result[:], ALU.add).then_inc(s["softplus_step"], 1)
            dve.wait_ge(s["softplus_step"], 13)
            nc.vector.tensor_tensor(result[:], ratio[:], positive[:], ALU.add).then_inc(s["softplus_step"], 1)
            dve.wait_ge(s["softplus_step"], 14)
            nc.vector.tensor_scalar(decay[:, 0, :], result[:], -8.0, None, ALU.mult).then_inc(s["softplus_step"], 1)
            dve.wait_ge(s["softplus_step"], 15)
            nc.vector.tensor_scalar(decay[:, 1, :], result[:], -4.0, None, ALU.mult).then_inc(s["softplus_step"], 1)

            for r in range(4):
                dve.wait_ge(c_all_in[r], 16)
                nc.vector.tensor_reduce(sums[:, r * QUARTER * RH:(r + 1) * QUARTER * RH],
                                        c_all[:, r * QUARTER:(r + 1) * QUARTER, :]
                                        .rearrange("p n (h d) -> p (n h) d", h=RH), AX_X, ALU.add)\
                    .then_inc(s["summed"], 1)
            dve.wait_ge(s["turned"], 2)
            for h in range(2):
                last = nc.vector.tensor_reduce(row_max[:, h, :], t_ps[h][:].rearrange("p (b t) -> p b t", b=2),
                                               AX_X, ALU.max)
            last.then_inc(s["maxed"], 1)
            dve.wait_ge(s["maxed"], 1)
            for h in range(2):
                last = nc.vector.tensor_tensor(shifted[:, h, :, :], t_ps[h][:].rearrange("p (b t) -> p b t", b=2),
                                               row_max[:, h, :].unsqueeze(2).to_broadcast([P, 2, CH]), ALU.subtract)
            last.then_inc(s["shifted_done"], 1)
            dve.wait_ge(s["exp_done"], 1)
            nc.vector.tensor_reduce(total[:], exps[:], AX_X, ALU.add).then_inc(s["totalled"], 1)
            dve.wait_ge(s["totalled"], 1)
            nc.vector.reciprocal(row_max[:], total[:]).then_inc(s["inverted"], 1)
            dve.wait_ge(s["inverted"], 1)
            nc.vector.tensor_tensor(attn_t[:], exps[:], row_max[:].unsqueeze(3).to_broadcast([P, 2, 2, CH]), ALU.mult)\
                .then_inc(s["attn_done"], 1)

            dve.wait_ge(s["turned_back"], 2)
            for h in range(2):
                last = nc.vector.tensor_copy(attn[:, h * P:(h + 1) * P], t_ps[h][:])
            last.then_inc(s["attn_taken"], 1)
            dve.wait_ge(s["attn_taken"], 1)
            for r in range(4):
                part = c_all[:, r * QUARTER:(r + 1) * QUARTER, :].rearrange("p n (h d) -> p (n h) d", h=RH)
                nc.vector.tensor_tensor(part, part, attn[:, r * QUARTER * RH:(r + 1) * QUARTER * RH].unsqueeze(2)
                                        .to_broadcast([P, QUARTER * RH, D // RH]), ALU.mult).then_inc(s["weighted"], 1)
            dve.wait_ge(s["pooled_done"], 1)
            nc.vector.tensor_copy(pooled[:], hp_ps[:]).then_inc(s["taken"], 1)
            dve.wait_ge(s["taken"], 1)

        @block.scalar
        def _(act):
            act.wait_ge(s["softplus_step"], 2)
            nc.scalar.activation(u[:], magnitude[:], ACT.Exp, scale=-1.0).then_inc(s["softplus_step"], 1)
            act.wait_ge(s["softplus_step"], 6)
            nc.scalar.activation(logged[:], one_more[:], ACT.Ln).then_inc(s["softplus_step"], 1)
            act.wait_ge(s["shifted_done"], 1)
            nc.scalar.activation(exps[:], shifted[:], ACT.Exp, scale=RH / D).then_inc(s["exp_done"], 1)

        @block.tensor
        def _(pe):
            for h in range(2):
                pe.wait_ge(s["summed"], 2 * h + 2)
                nc.tensor.transpose(t_ps[h][:], sums[:, h * P:(h + 1) * P], ident[:]).then_inc(s["turned"], 1)
            pe.wait_ge(s["attn_done"], 1)
            for h in range(2):
                nc.tensor.transpose(t_ps[h][:], attn_t[:, h, :, :], ident[:]).then_inc(s["turned_back"], 1)
            pe.wait_ge(small_in, 32)
            for n in range(TILES):
                if n % QUARTER == 0:
                    pe.wait_ge(s["weighted"], n // QUARTER + 1)
                for h in range(2):
                    last = nc.tensor.matmul(hp_ps[:, h, 2 * n:2 * n + 2], c_all[:, n, h * P:(h + 1) * P],
                                            batch_ones[:], start=True, stop=True)
            last.then_inc(s["pooled_done"], 1)


def recurrent_gate(nc, dram, x, ident, tanh_gain, pooled, decay, rotated):
    FWHT_CHUNKS = FF2 // P
    with ExitStack() as ctx:
        def sb(name, shape, dt=F32):
            return ctx.enter_context(nc.sbuf_tensor(name, shape, dt))

        def ps(name, shape, dt=F32):
            return ctx.enter_context(nc.psum_tensor(name, shape, dt))

        def sem(name):
            return nc.alloc_semaphore(name)

        w_all = sb("gate_w", [P, 2, 2, P])
        w_hi = sb("gate_w_hi", [P, 2, 2, P], F32R)
        w_lo = sb("gate_w_lo", [P, 2, 2, P], F32R)
        bias = sb("gate_bias", [P, 2, 2])
        half_bias = sb("half_bias", [P, 2, 2])
        ones = sb("gate_ones", [P, 1])
        xn = sb("gate_xn", [P, GT, D])
        stats = sb("gate_stats", [P, GT, 6])
        mean_var = sb("gate_mean_var", [P, GT, 2])
        var_eps = sb("gate_var_eps", [P, GT])
        rstd = sb("gate_rstd", [P, GT])
        half = sb("gate_half", [P, GT])
        xt_hi = sb("gate_xt_hi", [P, 2, GROUP], F32R)
        xt_lo = sb("gate_xt_lo", [P, 2, GROUP], F32R)
        tanh_x = sb("tanh_x", [P, 2, GROUP])
        tanh_a = sb("tanh_a", [P, 2, GROUP])
        gated = sb("gated", [P, 2, BATCH * CH])
        a_all = sb("a_all", [P, 2, BATCH * CH])
        rest = sb("rest", [P, 2, BATCH * CH])
        from_pool = [sb(f"from_pool{r}", [P, 2, GROUP]) for r in range(2)]
        y_t = [sb(f"y_t{r}", [P, 2, GROUP]) for r in range(2)]
        w2 = [sb(f"w2_{r}", [P, FWHT_CHUNKS, D]) for r in range(2)]
        hadamard = sb("hadamard", [P, P])

        t_ps = [ps(f"gate_t_ps{r}", [P, GROUP]) for r in range(2)]
        z_ps = [ps(f"z_ps{r}", [P, 2, GROUP]) for r in range(2)]
        y_ps = [ps(f"gate_y_ps{r}", [P, 2, D]) for r in range(2)]

        small_in, w2_in, stored = sem("gate_small_in"), sem("w2_in"), sem("rotated_stored")
        s = {name: sem("gate_" + name) for name in
             "w_high w_split bias_ready half_set stats_raw stats_done eps_added rstd_ready xn_ready turned hi_taken "
             "all_taken lo_taken z_done tanh_done a_done squared gated_ready rest_ready rooted product_done pool_done "
             "y_ready y_turned x_updated butterflies rotated_done rotated_taken".split()}
        block = ctx.enter_context(nc.Block())

        def by_pairs(eng, body):
            for g in range(2):
                body(g, g)
            with eng.Fori(1, GROUPS // 2) as i:
                for r in range(2):
                    body(2 * i + r, r)

        def cols(buffer, g):
            return buffer[:, :, g * GROUP:(g + 1) * GROUP] if isinstance(g, int) \
                else buffer[:, :, bass.ds(g * GROUP, GROUP)]

        def col(buffer, kc, g):
            return buffer[:, kc, g * GROUP:(g + 1) * GROUP] if isinstance(g, int) \
                else buffer[:, kc, bass.ds(g * GROUP, GROUP)]

        def tile(g, t):
            return x[:, GT * g + t, :] if isinstance(g, int) else x[:, bass.ds(GT * g + t, 1), :]

        def flat(ap, g):
            return ap if isinstance(g, int) else ap.unsqueeze(1)

        @block.sync
        def _(sp):
            sp.dma_start(w_all[:], dram["gate_blocks"]).then_inc(small_in, 16)
            sp.dma_start(bias[:], dram["gate_bias"]).then_inc(small_in, 16)
            sp.dma_start(hadamard[:], dram["hadamard"]).then_inc(small_in, 16)
            sp.dma_start(w2[0][:], dram["w2_rows"]).then_inc(w2_in, 16)
            sp.wait_ge(s["rotated_taken"], 4)
            sp.dma_start(rotated, w2[0][:].rearrange("p c d -> p (c d)")).then_inc(stored, 16)
            sp.wait_ge(stored, 16)

        @block.gpsimd
        def _(pool):
            nc.gpsimd.memset(half[:], -0.5).then_inc(s["half_set"], 1)
            pool.wait_ge(s["half_set"], 1)

            def rstd_of(g):
                pool.wait_ge(s["stats_done"], g + 1)
                wait_count(pool, s["xn_ready"], g)
                wait_alone(pool)
                nc.gpsimd.tensor_scalar(var_eps[:].unsqueeze(2), mean_var[:, :, 1:2], EPS, None, ALU.add)\
                    .then_inc(s["eps_added"], 1)
                pool.wait_ge(s["eps_added"], g + 1)
                nc.gpsimd.tensor_tensor(rstd[:], var_eps[:], half[:], ALU.pow).then_inc(s["rstd_ready"], 1)

            rstd_of(0)
            with pool.Fori(1, GROUPS) as g:
                rstd_of(g)
            def scale_pooled(g, r):
                wait_count(pool, s["y_ready"], g - 1)
                for kc in range(2):
                    at = bass.ds(g * (GROUP // CH), GROUP // CH)
                    last = nc.gpsimd.tensor_tensor(
                        from_pool[r][:, kc, :].rearrange("p (b t) -> p b t", t=CH),
                        col(a_all, kc, g).rearrange("p (b t) -> p b t", t=CH),
                        pooled[:, kc, at].unsqueeze(2).to_broadcast([P, GROUP // CH, CH]), ALU.mult)
                last.then_inc(s["pool_done"], 1)

            pool.wait_ge(s["a_done"], 2 * GROUPS)
            by_pairs(pool, scale_pooled)

        @block.vector
        def _(dve):
            def stats_of(g):
                for t in range(GT):
                    last = nc.vector.bn_stats(stats[:, t, :], tile(g, t))
                last.then_inc(s["stats_raw"], 1)
                dve.wait_ge(s["stats_raw"], g + 1)
                wait_count(dve, s["eps_added"], g)
                wait_count(dve, s["xn_ready"], g)
                wait_alone(dve)
                for t in range(GT):
                    last = nc.vector.bn_aggr(mean_var[:, t, :], stats[:, t, :])
                last.then_inc(s["stats_done"], 1)

            def norm_of(g):
                dve.wait_ge(s["rstd_ready"], g + 1)
                wait_count(dve, s["turned"], 2 * g)
                for t in range(GT):
                    last = nc.vector.tensor_scalar(flat(xn[:, t, :], g), tile(g, t), mean_var[:, t, 0:1],
                                                   rstd[:, t:t + 1], ALU.subtract, ALU.mult)
                last.then_inc(s["xn_ready"], 1)

            def low_of(g):
                wait_count(dve, s["z_done"], 2 * g)
                for kc in range(2):
                    dve.wait_ge(s["all_taken"], 2 * g + kc + 1)
                    nc.vector.tensor_tensor(xt_lo[:, kc, :], col(gated, kc, g), xt_hi[:, kc, :].bitcast(F32),
                                            ALU.subtract).then_inc(s["lo_taken"], 1)

            dve.wait_ge(small_in, 48)
            nc.vector.memset(ones[:], 1.0)
            nc.vector.tensor_scalar(half_bias[:], bias[:], 0.5, None, ALU.mult).then_inc(s["bias_ready"], 1)
            nc.vector.tensor_copy(w_hi[:], w_all[:]).then_inc(s["w_high"], 1)
            dve.wait_ge(s["w_high"], 1)
            nc.vector.tensor_tensor(w_lo[:], w_all[:], w_hi[:].bitcast(F32), ALU.subtract).then_inc(s["w_split"], 1)

            def use(g):
                dve.wait_ge(s["tanh_done"], 2 * g + 2)
                dve.wait_ge(s["all_taken"], 2 * g + 2)
                nc.vector.scalar_tensor_tensor(out=cols(gated, g), in0=tanh_x[:], scalar=1.0, in1=cols(gated, g),
                                               op0=ALU.add, op1=ALU.mult).then_inc(s["gated_ready"], 1)
                dve.wait_ge(s["squared"], 2 * g + 2)
                nc.vector.tensor_scalar(cols(rest, g), cols(rest, g), 1.0, None, ALU.min).then_inc(s["rest_ready"], 1)

            stats_of(0)
            norm_of(0)
            low_of(0)
            with dve.Fori(0, GROUPS - 1) as g:
                stats_of(g + 1)
                norm_of(g + 1)
                use(g)
                low_of(g + 1)
            use(GROUPS - 1)

            dve.wait_ge(w2_in, 16)
            for n, span in enumerate((1, 2, 4)):
                src = w2[n % 2][:].rearrange("p (a two b) d -> p a two (b d)", two=2, b=span)
                dst = w2[1 - n % 2][:].rearrange("p (a two b) d -> p a two (b d)", two=2, b=span)
                for k, op in enumerate((ALU.add, ALU.subtract)):
                    last = nc.vector.tensor_tensor(dst[:, :, k, :], src[:, :, 0, :], src[:, :, 1, :], op)
                last.then_inc(s["butterflies"], 1)
                dve.wait_ge(s["butterflies"], n + 1)

            def finish(g, r):
                dve.wait_ge(s["rooted"], g + 1)
                wait_count(dve, s["y_turned"], 2 * g - 2)
                nc.vector.scalar_tensor_tensor(out=y_t[r][:], in0=cols(gated, g), scalar=0.5, in1=cols(rest, g),
                                               op0=ALU.mult, op1=ALU.mult).then_inc(s["product_done"], 1)
                dve.wait_ge(s["product_done"], g + 1)
                dve.wait_ge(s["pool_done"], g + 1)
                nc.vector.tensor_tensor(y_t[r][:], y_t[r][:], from_pool[r][:], ALU.add).then_inc(s["y_ready"], 1)
                for t in range(2):
                    dve.wait_ge(s["y_turned"], 2 * g + t + 1)
                    rows = x[:, bass.ds(GT * g + 2 * t, 2), :]
                    nc.vector.scalar_tensor_tensor(out=rows, in0=y_ps[t][:], scalar=tanh_gain[:, 2:3], in1=rows,
                                                   op0=ALU.mult, op1=ALU.add).then_inc(s["x_updated"], 1)

            dve.wait_ge(s["gated_ready"], GROUPS)
            by_pairs(dve, finish)

        @block.scalar
        def _(act):
            act.wait_ge(s["bias_ready"], 1)

            def take(g):
                for kc in range(2):
                    act.wait_ge(s["turned"], 2 * g + kc + 1)
                    wait_count(act, s["z_done"], 2 * g)
                    nc.scalar.copy(xt_hi[:, kc, :], t_ps[kc][:]).then_inc(s["hi_taken"], 1)
                    nc.scalar.copy(col(gated, kc, g), t_ps[kc][:]).then_inc(s["all_taken"], 1)

            def gates(g):
                for kc in range(2):
                    act.wait_ge(s["z_done"], 2 * g + kc + 1)
                    if kc == 0:
                        wait_count(act, s["gated_ready"], g)
                    nc.scalar.activation(tanh_a[:, kc, :], z_ps[kc][:, 1, :], ACT.Tanh, bias=half_bias[:, kc, 1:2],
                                         scale=0.5)
                    nc.scalar.activation(tanh_x[:, kc, :], z_ps[kc][:, 0, :], ACT.Tanh, bias=half_bias[:, kc, 0:1],
                                         scale=0.5).then_inc(s["tanh_done"], 1)
                for kc in range(2):
                    act.wait_ge(s["tanh_done"], 2 * g + 2)
                    nc.scalar.activation(col(a_all, kc, g), tanh_a[:, kc, :], ACT.Exp, bias=decay[:, 1, kc:kc + 1],
                                         scale=decay[:, 1, kc:kc + 1]).then_inc(s["a_done"], 1)
                    nc.scalar.activation(col(rest, kc, g), tanh_a[:, kc, :], ACT.Exp, bias=decay[:, 0, kc:kc + 1],
                                         scale=decay[:, 0, kc:kc + 1]).then_inc(s["squared"], 1)

            take(0)
            gates(0)
            take(1)
            with act.Fori(1, GROUPS - 1) as g:
                gates(g)
                take(g + 1)
            gates(GROUPS - 1)
            for n in range(4):
                act.wait_ge(s["rotated_done"], n + 1)
                nc.scalar.mul(w2[0][:, 2 * n:2 * n + 2, :], (t_ps[n % 2])[:].rearrange("p (c d) -> p c d", c=2),
                              float(FF2) ** -0.5).then_inc(s["rotated_taken"], 1)
            act.wait_ge(s["rest_ready"], GROUPS)
            with act.Fori(0, GROUPS) as g:
                nc.scalar.activation(cols(rest, g), cols(rest, g), ACT.Sqrt, bias=ones[:], scale=-1.0)\
                    .then_inc(s["rooted"], 1)

        @block.tensor
        def _(pe):
            def turn(g):
                pe.wait_ge(s["xn_ready"], g + 1)
                wait_count(pe, s["lo_taken"], 2 * g)
                wait_count(pe, s["all_taken"], 2 * g)
                for kc in range(2):
                    for t in range(GT):
                        last = nc.tensor.transpose(t_ps[kc][:, t * P:(t + 1) * P], xn[:, t, kc * P:(kc + 1) * P], ident[:])
                    last.then_inc(s["turned"], 1)

            def gates(g):
                for kc in range(2):
                    pe.wait_ge(s["lo_taken"], 2 * g + kc + 1)
                    wait_count(pe, s["tanh_done"], 2 * g)
                    for gate in range(2):
                        for t, (w, xt) in enumerate(((w_hi, xt_hi), (w_lo, xt_hi), (w_hi, xt_lo))):
                            last = nc.tensor.matmul(z_ps[kc][:, gate, :], w[:, kc, gate, :], xt[:, kc, :],
                                                    start=(t == 0), stop=(t == 2))
                    last.then_inc(s["z_done"], 1)

            turn(0)
            pe.wait_ge(s["w_split"], 1)
            gates(0)
            turn(1)
            with pe.Fori(1, GROUPS - 1) as g:
                gates(g)
                turn(g + 1)
            gates(GROUPS - 1)
            pe.wait_ge(s["butterflies"], 3)
            pe.wait_ge(s["all_taken"], 2 * GROUPS)
            for n in range(4):
                wait_count(pe, s["rotated_taken"], n - 1)
                nc.tensor.matmul(t_ps[n % 2][:], hadamard[:], w2[1][:, 2 * n:2 * n + 2, :].rearrange("p c d -> p (c d)"),
                                 start=True, stop=True).then_inc(s["rotated_done"], 1)
            def turn_back(g, r):
                pe.wait_ge(s["y_ready"], g + 1)
                for t in range(2):
                    wait_count(pe, s["x_updated"], 2 * g + t - 1)
                    for a in range(2):
                        for kc in range(2):
                            at = (2 * t + a) * P
                            last = nc.tensor.transpose(y_ps[t][:, a, kc * P:(kc + 1) * P],
                                                       y_t[r][:, kc, at:at + P], ident[:])
                    last.then_inc(s["y_turned"], 1)

            by_pairs(pe, turn_back)


def program(nc, dram, out, stages="amrf", start=None):
    with ExitStack() as ctx:
        x = ctx.enter_context(nc.sbuf_tensor("x_sb", [P, TILES, D], F32))
        ident = ctx.enter_context(nc.sbuf_tensor("ident", [P, P], F32))
        gains = ctx.enter_context(nc.sbuf_tensor("gains", [P, 4], F32))
        tanh_gain = ctx.enter_context(nc.sbuf_tensor("tanh_gain", [P, 4], F32))
        tanh_ready = ctx.enter_context(nc.semaphore("tanh_ready"))
        ident_in = ctx.enter_context(nc.semaphore("ident_in"))
        x_in = ctx.enter_context(nc.semaphore("x_in"))
        stored = ctx.enter_context(nc.semaphore("stored"))
        with nc.Block() as block:
            @block.sync
            def _(sp):
                sp.dma_start(ident[:], dram["ident"]).then_inc(ident_in, 16)
                sp.dma_start(gains[:], dram["gains"]).then_inc(ident_in, 16)
                if "a" not in stages:
                    sp.dma_start(x[:], dram["x"].rearrange("(n b) c t -> (b c) n t", b=2)).then_inc(x_in, 16)
                    sp.wait_ge(x_in, 16)

            @block.scalar
            def _(act):
                act.wait_ge(ident_in, 32)
                nc.scalar.activation(tanh_gain[:], gains[:], ACT.Tanh).then_inc(tanh_ready, 1)
                act.wait_ge(tanh_ready, 1)
        if "a" in stages:
            with nc.cleanup_on_exit():
                attention(nc, dram, x, ident, tanh_gain)
        if "m" in stages:
            with nc.cleanup_on_exit():
                feed_forward(nc, dram, x, ident, tanh_gain, 1, FF, EXPERTS + 1, dram["experts"], True)
        rotated = nc.dram_tensor("rotated", (P, FF2 // P * D), F32, kind="Internal").ap()
        if "r" in stages:
            with nc.cleanup_on_exit(), ExitStack() as gate_ctx:
                pooled = gate_ctx.enter_context(nc.sbuf_tensor("pooled", [P, 2, BATCH], F32))
                decay = gate_ctx.enter_context(nc.sbuf_tensor("decay", [P, 2, 2], F32))
                pooled_context(nc, dram, ident, pooled, decay)
                recurrent_gate(nc, dram, x, ident, tanh_gain, pooled, decay, rotated)
        if "f" in stages:
            feed_forward(nc, dram, x, ident, tanh_gain, 3, FF2, 1, [dram["w13"][0], dram["w13"][1], rotated], False, out)
        else:
            with nc.Block() as block:
                @block.sync
                def _(sp):
                    sp.dma_start(out.rearrange("(n b) c t -> (b c) n t", b=2), x[:]).then_inc(stored, 16)
                    sp.wait_ge(stored, 16)


def layouts(a):
    a = {name: np.asarray(v) for name, v in a.items()}
    batch_of, ch_of, d_of = column_order()
    swap = ch_of - d_of + np.where(d_of < 4, d_of ^ 2, d_of)

    def per_batch(w_t, cols, batch):
        w = np.zeros((2, CH, P), np.float32)
        for b in range(2):
            w[b][:, batch == b] = w_t[:, cols[batch == b]]
        return w.reshape(P, P)

    plain, plain_batch = np.tile(np.arange(CH), 2), np.repeat(np.arange(2), CH)
    wq, wk, wv, wo = (a[f"L0_xattn_W{m}"].T for m in "qkvo")
    bq, bk, bv, bo = (a[f"L0_xattn_b{m}"] for m in "qkvo")
    own = np.zeros((P, UH), np.float32)
    own[96 + np.arange(8), np.arange(8) % UH] = 1
    out = {
        "x": a["x"], "ctx_2048": a["ctx_2048"],
        "ident": np.eye(P, dtype=np.float32),
        "w_in": np.stack([per_batch(wq, ch_of, batch_of), per_batch(wq, swap, batch_of),
                          per_batch(wk, ch_of, batch_of), per_batch(wk, swap, batch_of),
                          per_batch(wv, plain, plain_batch)], 1),
        "w_out": per_batch(wo, plain, plain_batch),
        "bias": np.stack([bq[ch_of], bq[swap], bk[ch_of], bk[swap], bo[plain]], 1),
        "bias_v": np.broadcast_to(bv[plain], (P, P)),
        "rope": np.stack(rotary_tables(), 1),
        "own_head": own,
        "gains": np.broadcast_to(np.stack([a["g_xattn"][0], a["g_ffn"][0], a["g_xattn"][1], a["g_ffn"][1]]), (P, 4)),
    }

    def pieces(gate_up, down):
        return np.concatenate([gate_up.reshape(2, P, -1),
                               down.reshape(-1, P, D).transpose(1, 0, 2).reshape(1, P, -1)])

    gate_up = [a["L0_ffn_shared_gate_up"], *a["L0_ffn_w_gate_up"]]
    down = [a["L0_ffn_shared_down"], *a["L0_ffn_w_down"]]
    out["experts"] = np.stack([pieces(g, d) for g, d in zip(gate_up, down)])
    out["w13"] = np.concatenate([a["L1_ffn_W1"].T, a["L1_ffn_W3"].T], 1).reshape(2, P, 2 * FF2)
    out["w2_rows"] = a["L1_ffn_W2"].T.reshape(FF2 // P, P, D).transpose(1, 0, 2)
    hadamard = np.ones((1, 1), np.float32)
    while len(hadamard) < P:
        hadamard = np.block([[hadamard, hadamard], [hadamard, -hadamard]])
    out["hadamard"] = hadamard
    blocks = np.zeros((2, P, 2, P), np.float32)
    for gate, w in enumerate((a["L1_xattn_w_input"], a["L1_xattn_w_a"])):
        for h in range(8):
            at = h % 4 * 32
            blocks[h // 4, at:at + 32, gate, at:at + 32] = w[h]
    out["gate_blocks"] = blocks.transpose(1, 0, 2, 3)
    out["gate_bias"] = np.stack([a["L1_xattn_b_input"].reshape(2, P), a["L1_xattn_b_a"].reshape(2, P)], 1).transpose(2, 0, 1)
    out["a_param"] = a["L1_xattn_a_param"].reshape(2, P).T
    out["batch_ones"] = np.repeat(np.eye(2, dtype=np.float32), CH, 0)
    out["router"] = a["L0_ffn_gate_w"].reshape(2, P, EXPERTS).transpose(1, 0, 2)
    out["earlier"] = np.broadcast_to(np.tril(np.ones((EXPERTS, EXPERTS), np.float32), -1), (P, EXPERTS, EXPERTS))
    return {name: np.ascontiguousarray(v) for name, v in out.items()}


def kernel(**inputs):
    import concourse.bacc as bacc
    from concourse.bass_utils import run_bass_kernel_spmd

    arrays = layouts(inputs)
    nc = bacc.Bacc("TRN2", target_bir_lowering=False, num_devices=1)
    dram = {name: nc.dram_tensor(f"in_{name}", v.shape, mybir.dt.from_np(v.dtype), kind="ExternalInput").ap()
            for name, v in arrays.items()}
    out = nc.dram_tensor("out", (BATCH, CH, D), F32, kind="ExternalOutput").ap()
    program(nc, dram, out)
    done = run_bass_kernel_spmd(nc, [{f"in_{name}": v for name, v in arrays.items()}], core_ids=[0])
    return done.results[0]["out"]
```

```python
from contextlib import ExitStack

import numpy as np

import concourse.bass as bass
from concourse import mybir

F32 = mybir.dt.float32
F32R = mybir.dt.float32r
ACT = mybir.ActivationFunctionType
ALU = mybir.AluOpType
AX_X = mybir.AxisListType.X

P = 128
BATCH, CH, D = 64, 64, 256
TILES = BATCH * CH // P
HEADS, DH = 8, 8
UNITS, UH = 4, 4
EXPERTS, FF = 8, 512
FF2 = 1024
GROUP = 512
GT = GROUP // P
GROUPS = BATCH * CH // GROUP
EPS = 1e-5
RING = 4


def column_order():
    j, d, u = np.meshgrid(range(UH), range(DH), range(UNITS), indexing="ij")
    return (u // 2).ravel(), ((u % 2 * UH + j) * DH + d).ravel(), d.ravel()


def rotary_tables():
    theta = np.float32(1.0) / np.float32(10000.0) ** (np.arange(0, 4, 2, dtype=np.float32) / np.float32(4))
    angle = np.arange(D, dtype=np.float32)[None, :] * theta[:, None].astype(np.float32)
    d = column_order()[2]
    rotated = (d < 4)[:, None]
    cos = np.where(rotated, np.cos(angle)[d % 2], 1).astype(np.float32)
    sin = np.where(rotated, np.where(d < 2, -1, 1)[:, None] * np.sin(angle)[d % 2], 0).astype(np.float32)
    return cos, sin


def wait_count(eng, sem, count):
    if not (isinstance(count, int) and count <= 0):
        eng.wait_ge(sem, count)


def wait_alone(eng):
    eng.nop(nofuse=True)


def attention(nc, dram, x, ident, tanh_gain):
    HP = 2 * HEADS
    LAG = 8
    ROWS, MROWS = 96, 104
    PEEL_FIRST, PEEL_LAST = (-2, -1, 0, 1), (30, 31, 32, 33)

    with ExitStack() as ctx:
        def sb(name, shape, dt=F32):
            return ctx.enter_context(nc.sbuf_tensor(name, shape, dt))

        def ps(name, shape, dt=F32):
            return ctx.enter_context(nc.psum_tensor(name, shape, dt))

        def sem(name):
            return nc.alloc_semaphore(name)

        w_in = sb("w_in", [P, 5, P])
        w_out = sb("w_out", [P, P])
        bias = sb("bias", [P, 5])
        bias_v = sb("bias_v", [P, P])
        rope = sb("rope", [P, 2, D])
        own_head = sb("own_head", [P, UH])
        gains = sb("gains", [P, 4])
        out_bias = sb("out_bias", [P, 1])
        half = sb("half", [P, 1])

        c_in = [sb(f"c_in{r}", [P, D]) for r in range(RING)]
        stats = sb("stats", [P, 6])
        mean_var = sb("mean_var", [P, 2])
        var_eps = sb("var_eps", [P, 1])
        rstd = sb("rstd", [P, 1])
        xn = sb("xn", [P, D])
        roped = {a: sb(f"{a}_roped", [P, 2, D]) for a in "qk"}
        whole = {a: sb(f"{a}_whole", [P, D]) for a in "qk"}
        part = {a: sb(f"{a}_part", [P, 2, D], F32R) for a in "qk"}
        q_st = [sb(f"q_st{r}", [P, UNITS, D], F32R) for r in range(RING)]
        k_st = [sb(f"k_st{r}", [P, UNITS, UH, D], F32R) for r in range(RING)]
        v_st = [sb(f"v_st{r}", [P, 2, HP, 32]) for r in range(RING)]
        row_max = [sb(f"row_max{r}", [P, 2 * HP]) for r in range(2)]
        m_parts = sb("m_parts", [P, 4 * HP])
        m_rows = sb("m_rows", [4 * HP, P], F32R)
        e_t = [sb(f"e_t{r}", [P, 2, D]) for r in range(8)]
        o_sb = [sb(f"o_sb{r}", [P, 2, D]) for r in range(2)]
        o_rcp = sb("o_rcp", [P, HP])
        a_sb = sb("a_sb", [P, 2, 2, CH])
        a_t = sb("a_t", [P, D])
        y_sb = sb("y_sb", [P, D])

        s_ps = [ps(f"s_ps{r}", [P, 4, D]) for r in range(2)]
        st_ps = [ps(f"st_ps{r}", [P, 2, D]) for r in range(2)]
        o_ps = ps("o_ps", [P, 2, D])
        misc = ps("misc", [P, 512])

        consts_in, more_consts_in = sem("consts_in"), sem("more_consts_in")
        x_first_in, x_rest_in = sem("x_first_in"), sem("x_rest_in")
        c_loaded = [sem(f"c_loaded{r}") for r in range(RING)]
        q_stacked = [sem(f"q_stacked{r}") for r in range(RING)]
        k_stacked = [[sem(f"k_stacked{j}_{r}") for r in range(RING)] for j in range(UH // 2)]
        m_stacked = [sem(f"m_stacked{r}") for r in range(RING)]
        names = ("values_cleared first_cleared others_cleared ones_set own_set tanh_ready bias_ready half_set "
                 "stats_raw stats_done eps_added rstd_ready xn_ready "
                 "q_projected q_roped q_summed q_high q_split k_projected k_roped k_summed k_high k_split "
                 "v_projected v_stored scored max_taken m_high m_split m_turned m_taken "
                 "st_scored exp_done pv_done o_taken o_turned rcp_ready o_normed a_turned a_taken "
                 "y_projected y_taken y_free").split()
        s = {name: sem(name) for name in names}

        def steps(eng, body, before_loop=None, after_first=None):
            for n in PEEL_FIRST:
                body(n, n, 0)
                if n == PEEL_FIRST[0] and after_first:
                    after_first()
            if before_loop:
                before_loop()
            with eng.Fori(0, (PEEL_LAST[0] - PEEL_FIRST[-1] - 1) // RING) as i:
                for c in range(PEEL_FIRST[-1] + 1, PEEL_FIRST[-1] + 1 + RING):
                    body(i * RING + c, c, i)
            for n in PEEL_LAST:
                body(n, n, 0)

        def there(n, c, k):
            return not isinstance(n, int) or 0 <= n + k < TILES

        def uses(c, i, k):
            return i + (c + k) // RING + 1

        def st_head(s_):
            return (0, s_ - LAG) if s_ >= LAG else (-1, s_ + LAG)

        block = ctx.enter_context(nc.Block())

        @block.sync
        def _(sp):
            rows = dram["x"].rearrange("(n b) c t -> (b c) n t", b=2)
            ctx_rows = dram["ctx_2048"].rearrange("(n b) c t -> n (b c) t", b=2)
            sp.dma_start(c_in[0][:], ctx_rows[0:1, :, :]).then_inc(c_loaded[0], 16)
            for dst, src in ((w_in[:], dram["w_in"]), (bias[:], dram["bias"]), (rope[:], dram["rope"]),
                             (own_head[:], dram["own_head"])):
                sp.dma_start(dst, src).then_inc(consts_in, 16)
            sp.dma_start(x[:, 0:4, :], rows[:, 0:4, :]).then_inc(x_first_in, 16)
            for dst, src in ((bias_v[:], dram["bias_v"]), (gains[:], dram["gains"]), (ident[:], dram["ident"]),
                             (w_out[:], dram["w_out"])):
                sp.dma_start(dst, src).then_inc(more_consts_in, 16)

            def body(n, c, i):
                if there(n, c, 3):
                    r = (c + 3) % RING
                    wait_count(sp, s["v_projected"], n)
                    sp.dma_start(c_in[r][:], ctx_rows[bass.ds(n + 3, 1), :, :] if not isinstance(n, int)
                                 else ctx_rows[n + 3:n + 4, :, :]).then_inc(c_loaded[r], 16)
                if isinstance(n, int) and n == -2:
                    for t in range(4, TILES, 14):
                        sp.dma_start(x[:, t:t + 14, :], rows[:, t:t + 14, :]).then_inc(x_rest_in, 16)
                if there(n, c, 0):
                    r = c % RING
                    sp.wait_ge(s["m_taken"], n + 1)
                    sp.dma_start(q_st[r][ROWS:MROWS, :, :].bitcast(F32),
                                 m_rows[:, :].bitcast(F32)).then_inc(m_stacked[r], 16)
                if there(n, c, 2):
                    r = (c + 2) % RING
                    wait_count(sp, s["st_scored"], HP * (n - 1))
                    wait_alone(sp)
                    if isinstance(n, int) and n == -2:
                        sp.wait_ge(s["first_cleared"], 2)
                    if isinstance(n, int) and n == 0:
                        sp.wait_ge(s["others_cleared"], 2)

                    def stack_k(j, t, of):
                        sp.dma_start(k_st[r][32 * t + 8 * j:32 * t + 8 * j + 8, :, j, :].bitcast(F32),
                                     part["k"][32 * j:32 * j + 32, of, :].bitcast(F32)).then_inc(k_stacked[j // 2][r], 16)

                    sp.wait_ge(s["k_high"], n + 3)
                    for j in range(2):
                        stack_k(j, 0, 0)
                        stack_k(j, 1, 0)
                    sp.wait_ge(s["k_split"], n + 3)
                    for j in range(2):
                        stack_k(j, 2, 1)
                    sp.wait_ge(s["q_split"], n + 3)
                    for t, of in enumerate((0, 1, 0)):
                        sp.dma_start(q_st[r][32 * t:32 * t + 32, :, :].bitcast(F32),
                                     part["q"][:, of, :].bitcast(F32)).then_inc(q_stacked[r], 16)
                    for j in range(2, UH):
                        for t, of in enumerate((0, 0, 1)):
                            stack_k(j, t, of)

            steps(sp, body)

        @block.gpsimd
        def _(pool):
            nc.gpsimd.memset(half[:], -0.5).then_inc(s["half_set"], 1)
            nc.gpsimd.memset(y_sb[:], 0.0).then_inc(s["y_free"], 1)
            for r in (0, 1):
                nc.gpsimd.memset(k_st[r][0:ROWS, :, :, :].bitcast(F32), 0.0).then_inc(s["first_cleared"], 1)
            pool.wait_ge(s["half_set"], 1)

            def body(n, c, i):
                if there(n, c, 2):
                    pool.wait_ge(s["stats_done"], n + 3)
                    wait_count(pool, s["xn_ready"], n + 2)
                    wait_alone(pool)
                    nc.gpsimd.tensor_scalar(var_eps[:], mean_var[:, 1:2], EPS, None, ALU.add).then_inc(s["eps_added"], 1)
                    pool.wait_ge(s["eps_added"], n + 3)
                    nc.gpsimd.tensor_tensor(rstd[:], var_eps[:], half[:], ALU.pow).then_inc(s["rstd_ready"], 1)
                if there(n, c, -2):
                    pool.wait_ge(s["y_taken"], n - 1)
                    row = x[:, n - 2, :] if isinstance(n, int) else x[:, bass.ds(n - 2, 1), :]
                    y = y_sb[:] if isinstance(n, int) else y_sb[:].rearrange("p (o t) -> p o t", o=1)
                    nc.gpsimd.tensor_tensor(row, row, y, ALU.add).then_inc(s["y_free"], 1)
                for a in "kq":
                    if there(n, c, 2):
                        r, before = (c + 2) % RING, (c + 1) % RING
                        stacked = {"q": [q_stacked], "k": k_stacked}[a]
                        pool.wait_ge(s[a + "_roped"], n + 3)
                        nc.gpsimd.tensor_tensor(whole[a][:], roped[a][:, 0, :], roped[a][:, 1, :], ALU.add)\
                            .then_inc(s[a + "_summed"], 1)
                        pool.wait_ge(s[a + "_summed"], n + 3)
                        if there(n, c, 1):
                            for of_ring in stacked:
                                pool.wait_ge(of_ring[before], (48 if a == "q" else 96) * uses(c, i, 1))
                        wait_alone(pool)
                        nc.gpsimd.tensor_copy(part[a][:, 0, :], whole[a][:]).then_inc(s[a + "_high"], 1)
                        pool.wait_ge(s[a + "_high"], n + 3)
                        nc.gpsimd.tensor_tensor(part[a][:, 1, :], whole[a][:], part[a][:, 0, :].bitcast(F32),
                                                ALU.subtract).then_inc(s[a + "_split"], 1)

            steps(pool, body)

        @block.vector
        def _(dve):
            def clear_values(rings):
                for r in rings:
                    nc.vector.memset(v_st[r][:], 0.0).then_inc(s["values_cleared"], 1)
                dve.wait_ge(s["values_cleared"], rings[-1] + 1)
                for r in rings:
                    nc.vector.memset(v_st[r][:, :, :, DH:DH + 1], 1.0).then_inc(s["ones_set"], 1)
                dve.wait_ge(s["ones_set"], rings[-1] + 1)

            clear_values((0,))
            nc.vector.memset(k_st[2][0:ROWS, :, :, :].bitcast(F32), 0.0).then_inc(s["others_cleared"], 1)
            dve.wait_ge(consts_in, 4 * 16)
            dve.wait_ge(x_first_in, 16)

            def rope_parts(a, n, c, cols):
                dve.wait_ge(s[a + "_projected"], n + 3)
                wait_count(dve, s[a + "_summed"], n + 2)
                for t in range(2):
                    last = nc.vector.scalar_tensor_tensor(
                        out=roped[a][:, t, :], in0=misc[:, t * D:(t + 1) * D], scalar=bias[:, cols + t:cols + t + 1],
                        in1=rope[:, t, :], op0=ALU.add, op1=ALU.mult)
                last.then_inc(s[a + "_roped"], 1)

            def body(n, c, i):
                for s_ in range(HP):
                    if s_ == 0 and there(n, c, 2):
                        row = x[:, n + 2, :] if isinstance(n, int) else x[:, bass.ds(n + 2, 1), :]
                        wait_count(dve, s["stats_done"], n + 2)
                        nc.vector.bn_stats(stats[:], row).then_inc(s["stats_raw"], 1)
                        dve.wait_ge(s["stats_raw"], n + 3)
                        wait_count(dve, s["xn_ready"], n + 2)
                        wait_count(dve, s["eps_added"], n + 2)
                        wait_alone(dve)
                        nc.vector.bn_aggr(mean_var[:], stats[:]).then_inc(s["stats_done"], 1)
                    if s_ == 0:
                        if there(n, c, 0):
                            dve.wait_ge(s["max_taken"], (n + 1) * (HP // 2))
                            wait_count(dve, s["m_turned"], n)
                            nc.vector.tensor_scalar(m_parts[:, 0:2 * HP].bitcast(F32R), row_max[c % 2][:], -1.0, None,
                                                    ALU.mult).then_inc(s["m_high"], 1)
                            dve.wait_ge(s["m_high"], n + 1)
                            nc.vector.scalar_tensor_tensor(out=m_parts[:, 2 * HP:4 * HP].bitcast(F32R),
                                                           in0=row_max[c % 2][:], scalar=-1.0,
                                                           in1=m_parts[:, 0:2 * HP], op0=ALU.mult,
                                                           op1=ALU.subtract).then_inc(s["m_split"], 1)
                    if s_ == 2 and there(n, c, 2):
                        rope_parts("k", n, c, 2)
                    if s_ == 4 and there(n, c, 2):
                        row = x[:, n + 2, :] if isinstance(n, int) else x[:, bass.ds(n + 2, 1), :]
                        out = xn[:] if isinstance(n, int) else xn[:].rearrange("p (o t) -> p o t", o=1)
                        dve.wait_ge(s["rstd_ready"], n + 3)
                        dve.wait_ge(s["stats_done"], n + 3)
                        wait_count(dve, s["q_projected"], n + 2)
                        nc.vector.tensor_scalar(out, row, mean_var[:, 0:1], rstd[:], ALU.subtract, ALU.mult)\
                            .then_inc(s["xn_ready"], 1)
                    if s_ == 6 and there(n, c, 2):
                        rope_parts("q", n, c, 0)
                    if s_ == 8 and there(n, c, 2):
                        r = (c + 2) % RING
                        if isinstance(n, int) and n == PEEL_FIRST[0]:
                            dve.wait_ge(more_consts_in, 4 * 16)
                        dve.wait_ge(s["v_projected"], n + 3)
                        wait_count(dve, s["pv_done"], UNITS * (n - 1))
                        for h in range(2):
                            last = nc.vector.tensor_tensor(
                                v_st[r][:, h, :, 0:DH], misc[:, h * P:(h + 1) * P].rearrange("p (h d) -> p h d", d=DH),
                                bias_v[:].rearrange("p (h d) -> p h d", d=DH), ALU.add)
                        last.then_inc(s["v_stored"], 1)
                    if s_ in (10, 12) and there(n, c, -1):
                        b = s_ // 12
                        o = misc[:, :].rearrange("p (h r) -> p h r", r=32)
                        k = 2 * (n - 1) + b
                        dve.wait_ge(s["o_turned"], k + 1)
                        nc.vector.reciprocal(o_rcp[:].unsqueeze(2), o[:, :, DH:DH + 1]).then_inc(s["rcp_ready"], 1)
                        dve.wait_ge(s["rcp_ready"], k + 1)
                        if b == 0:
                            wait_count(dve, s["a_turned"], n - 1)
                        nc.vector.tensor_tensor(
                            a_sb[:, :, b, :].rearrange("p h (j d) -> p h j d", d=DH),
                            o[:, :, 0:DH].rearrange("p (h j) d -> p h j d", h=2),
                            o_rcp[:].rearrange("p (h j) -> p h j", h=2).unsqueeze(3).to_broadcast([P, 2, HEADS, DH]),
                            ALU.mult).then_inc(s["o_normed"], 1)
                    if s_ % 2 == 0 and there(n, c, 1):
                        g = (n + 1) * (HP // 2) + s_ // 2
                        dve.wait_ge(s["scored"], g + 1)
                        if s_ == 0:
                            wait_count(dve, s["m_split"], n)
                        u, j = s_ // UH, s_ % UH
                        out = row_max[(c + 1) % 2][:].rearrange("p (j u h) -> p j u h", j=UH, u=UNITS)[:, j:j + 2, u, :]
                        nc.vector.tensor_reduce(out, s_ps[s_ // 2 % 2][:].rearrange("p (j h) t -> p j h t", j=2),
                                                AX_X, ALU.max).then_inc(s["max_taken"], 1)

            def prepare_rest():
                dve.wait_ge(s["tanh_ready"], 1)
                nc.vector.tensor_tensor(out_bias[:], tanh_gain[:, 0:1], bias[:, 4:5], ALU.mult)\
                    .then_inc(s["bias_ready"], 1)
                clear_values((1, 2, 3))
                nc.vector.memset(k_st[3][0:ROWS, :, :, :].bitcast(F32), 0.0).then_inc(s["others_cleared"], 1)

            steps(dve, body, lambda: dve.wait_ge(x_rest_in, 32), prepare_rest)

        @block.scalar
        def _(act):
            act.wait_ge(consts_in, 4 * 16)
            for r in range(RING):
                nc.scalar.copy(k_st[r][ROWS:MROWS, :, :, :],
                               own_head[ROWS:MROWS, :].unsqueeze(1).unsqueeze(3)
                               .to_broadcast([MROWS - ROWS, UNITS, UH, D])).then_inc(s["own_set"], 1)
                if r == 0:
                    act.wait_ge(more_consts_in, 4 * 16)
                    nc.scalar.activation(tanh_gain[:], gains[:], ACT.Tanh).then_inc(s["tanh_ready"], 1)
            act.wait_ge(s["bias_ready"], 1)

            def body(n, c, i):
                for s_ in range(HP):
                    if s_ == 14 and there(n, c, -1):
                        act.wait_ge(s["a_turned"], n)
                        wait_count(act, s["y_projected"], n - 1)
                        nc.scalar.copy(a_t[:], misc[:, 0:D]).then_inc(s["a_taken"], 1)
                    if s_ == 0 and there(n, c, -2):
                        act.wait_ge(s["y_projected"], n - 1)
                        act.wait_ge(s["y_free"], n - 1)
                        nc.scalar.activation(y_sb[:], misc[:, 0:D], ACT.Identity, bias=out_bias[:],
                                             scale=tanh_gain[:, 0:1]).then_inc(s["y_taken"], 1)
                    if s_ == 4 and there(n, c, 0):
                        act.wait_ge(s["m_turned"], n + 1)
                        if there(n, c, -1):
                            act.wait_ge(m_stacked[(c - 1) % RING], 16 * uses(c, i, -1))
                        nc.scalar.copy(m_rows[:], misc[0:4 * HP, 0:P]).then_inc(s["m_taken"], 1)
                    if s_ in (2, 10) and there(n, c, -1):
                        b = s_ // 10
                        act.wait_ge(s["pv_done"], UNITS * (n - 1) + 2 * b + 2)
                        wait_count(act, s["o_turned"], 2 * (n - 1) + b - 1)
                        nc.scalar.copy(o_sb[b][:], o_ps[:]).then_inc(s["o_taken"], 1)
                    k, h = st_head(s_)
                    if there(n, c, k):
                        g = HP * (n + k) + h
                        act.wait_ge(s["st_scored"], g + 1)
                        if h % UH == 0:
                            wait_count(act, s["pv_done"], UNITS * (n + k) + h // UH - 1)
                        nc.scalar.activation(e_t[h % 8][:], st_ps[h % 2][:], ACT.Exp, scale=float(DH) ** -0.5)\
                            .then_inc(s["exp_done"], 1)

            steps(act, body)

        @block.tensor
        def _(pe):
            pe.wait_ge(consts_in, 4 * 16)

            def project(a, n, c, at, rhs):
                for t in range(2):
                    last = nc.tensor.matmul(misc[:, t * D:(t + 1) * D], w_in[:, at + t, :], rhs,
                                            start=True, stop=True)
                last.then_inc(s[a + "_projected"], 1)

            def body(n, c, i):
                for s_ in range(HP):
                    if s_ == 0 and there(n, c, -2):
                        pe.wait_ge(s["a_taken"], n - 1)
                        nc.tensor.matmul(misc[:, 0:D], w_out[:], a_t[:], start=True, stop=True)\
                            .then_inc(s["y_projected"], 1)
                    if s_ == 2 and there(n, c, 2):
                        if isinstance(n, int) and n < 2:
                            wait_count(pe, s["v_stored"], n + 2)
                        else:
                            pe.wait_ge(s["y_taken"], n - 1)
                        pe.wait_ge(c_loaded[(c + 2) % RING], 16 * uses(c, i, 2))
                        project("k", n, c, 2, c_in[(c + 2) % RING][:])
                    if s_ == 4 and there(n, c, 0):
                        if isinstance(n, int) and n == 0:
                            pe.wait_ge(more_consts_in, 4 * 16)
                        if there(n, c, 2):
                            pe.wait_ge(s["k_roped"], n + 3)
                        else:
                            pe.wait_ge(s["y_taken"], n - 1)
                        pe.wait_ge(s["m_split"], n + 1)
                        wait_alone(pe)
                        nc.tensor.transpose(misc[0:4 * HP, 0:P], m_parts[:], ident[:]).then_inc(s["m_turned"], 1)
                    if s_ == 6 and there(n, c, 2):
                        pe.wait_ge(s["k_roped"], n + 3)
                        wait_count(pe, s["m_taken"], n + 1)
                        pe.wait_ge(s["xn_ready"], n + 3)
                        project("q", n, c, 0, xn[:])
                    if s_ == 8 and there(n, c, 2):
                        pe.wait_ge(s["q_roped"], n + 3)
                        for h in range(2):
                            last = nc.tensor.matmul(misc[:, h * P:(h + 1) * P],
                                                    c_in[(c + 2) % RING][:, h * P:(h + 1) * P], w_in[:, 4, :],
                                                    start=True, stop=True)
                        last.then_inc(s["v_projected"], 1)
                    if s_ in (10, 12) and there(n, c, -1):
                        b = s_ // 12
                        if b == 1:
                            pe.wait_ge(s["o_normed"], 2 * (n - 1) + 1)
                        elif there(n, c, 2):
                            pe.wait_ge(s["v_stored"], n + 3)
                        elif there(n, c, 0):
                            pe.wait_ge(s["m_taken"], n + 1)
                        else:
                            pe.wait_ge(s["y_taken"], n - 1)
                        pe.wait_ge(s["o_taken"], 2 * (n - 1) + b + 1)
                        for half_, u in ((h, u) for h in range(2) for u in range(2)):
                            at = (2 * half_ + u) * P
                            last = nc.tensor.transpose(misc[:, at:at + P], o_sb[b][:, u, half_ * P:(half_ + 1) * P],
                                                       ident[:])
                        last.then_inc(s["o_turned"], 1)
                    if s_ == 14 and there(n, c, -1):
                        pe.wait_ge(s["o_normed"], 2 * n)
                        for h in range(2):
                            last = nc.tensor.transpose(misc[:, h * P:(h + 1) * P], a_sb[:, h, :, :], ident[:])
                        last.then_inc(s["a_turned"], 1)

                    if s_ % 2 == 0 and there(n, c, 1):
                        r = (c + 1) % RING
                        g = (n + 1) * (HP // 2) + s_ // 2
                        if s_ == 0:
                            pe.wait_ge(q_stacked[r], 48 * uses(c, i, 1))
                        if s_ in (0, 2):
                            pe.wait_ge(k_stacked[s_ // 2][r], 96 * uses(c, i, 1))
                        wait_count(pe, s["max_taken"], g - 1)
                        for h in (s_, s_ + 1):
                            u, j = h // UH, h % UH
                            for half_ in range(2):
                                last = nc.tensor.matmul(s_ps[s_ // 2 % 2][:, 2 * (h - s_) + half_, :],
                                                        q_st[r][0:ROWS, u, half_ * P:(half_ + 1) * P],
                                                        k_st[r][0:ROWS, u, j, :], start=True, stop=True)
                        last.then_inc(s["scored"], 1)

                    k, h = st_head(s_)
                    if there(n, c, k):
                        r = (c + k) % RING
                        g = HP * (n + k) + h
                        if h == 0:
                            pe.wait_ge(m_stacked[r], 16 * uses(c, i, k))
                            if isinstance(n, int) and n == 0:
                                pe.wait_ge(s["own_set"], RING)
                        wait_count(pe, s["exp_done"], g - 1)
                        u, j = h // UH, h % UH
                        for half_ in range(2):
                            last = nc.tensor.matmul(st_ps[h % 2][:, half_, :],
                                                    k_st[r][0:MROWS, u, j, half_ * P:(half_ + 1) * P],
                                                    q_st[r][0:MROWS, u, :], start=True, stop=True)
                        last.then_inc(s["st_scored"], 1)

                    k, h = st_head((s_ - 2) % HP)
                    if s_ < 2:
                        k -= 1 if (s_ - 2) % HP >= LAG else 0
                    if h % UH == UH - 1 and there(n, c, k):
                        r = (c + k) % RING
                        u = h // UH
                        pe.wait_ge(s["exp_done"], HP * (n + k) + h + 1)
                        if u == 0:
                            pe.wait_ge(s["v_stored"], n + k + 1)
                        if u % 2 == 0:
                            wait_count(pe, s["o_taken"], 2 * (n + k) + u // 2)
                        for half_ in range(2):
                            for j in range(UH):
                                last = nc.tensor.matmul(o_ps[32 * j:32 * j + 32, u % 2, :],
                                                        v_st[r][:, half_, u * UH + j, :],
                                                        e_t[(u * UH + j) % 8][:, half_, :],
                                                        start=(half_ == 0), stop=(half_ == 1))
                        last.then_inc(s["pv_done"], 1)

            steps(pe, body)


def feed_forward(nc, dram, x, ident, tanh_gain, gain_at, hidden, passes, weights, routed, out=None):
    CHUNKS = hidden // P
    PIECE = 2 * hidden
    RINGS = 2 if passes > 1 else 1
    ROUTER = 8
    TURN_AT = CHUNKS - 1 if routed else CHUNKS - 2

    with ExitStack() as ctx:
        def sb(name, shape, dt=F32):
            return ctx.enter_context(nc.sbuf_tensor(name + tag, shape, dt))

        def ps(name, shape, dt=F32):
            return ctx.enter_context(nc.psum_tensor(name + tag, shape, dt))

        def sem(name):
            return nc.alloc_semaphore(name + tag)

        tag = "_moe" if routed else "_ffn"
        xt_hi = sb("xt_hi", [P, 2, BATCH * CH], F32R)
        xt_lo = sb("xt_lo", [P, 2, BATCH * CH], F32R)
        xn = sb("xn", [P, GT, D])
        stats = sb("stats", [P, GT, 6])
        mean_var = sb("mean_var", [P, GT, 2])
        var_eps = sb("var_eps", [P, GT])
        rstd = sb("rstd", [P, GT])
        half = sb("half", [P, GT])
        stage = [sb(f"stage{r}", [P, PIECE]) for r in range(2)]
        w_hi = [sb(f"w_hi{r}", [P, 3, PIECE], F32R) for r in range(RINGS)]
        w_lo = [sb(f"w_lo{r}", [P, 3, PIECE], F32R) for r in range(RINGS)]
        silu = [sb(f"silu{r}", [P, GROUP]) for r in range(2)]
        h_all = [sb(f"h_all{r}", [P, GROUP]) for r in range(2)]
        h_hi = sb("h_hi", [P, CHUNKS, GROUP], F32R)
        h_lo = sb("h_lo", [P, CHUNKS, GROUP], F32R)
        combine = sb("combine", [P, passes, TILES])
        now = sb("now", [P, GT])

        g_ps = [ps(f"g_ps{r}", [P, GROUP]) for r in range(2)]
        u_ps = [ps(f"u_ps{r}", [P, GROUP]) for r in range(2)]
        y_ps = ps("y_ps", [P, GT, D])
        t_ps = [ps(f"t_ps{r}", [P, GROUP]) for r in range(2)]

        piece_in = [sem(f"piece_in{r}") for r in range(2)]
        out_stored = sem("out_stored")
        names = ("stats_raw stats_done eps_added rstd_ready xn_ready half_set first_high first_split turned "
                 "hi_taken lo_taken w_high w_split "
                 "gate_done up_done silu_done product_done hi_done lo_done down_done shared_set now_set "
                 "added").split()
        s = {name: sem(name) for name in names}
        if routed:
            router_in = sem("router_in")
            router_w = sb("router_w", [P, 2, ROUTER])
            router_hi = sb("router_hi", [P, 2, ROUTER], F32R)
            router_lo = sb("router_lo", [P, 2, ROUTER], F32R)
            earlier = sb("earlier", [P, ROUTER, ROUTER])
            logits_t = sb("logits_t", [ROUTER, GROUP])
            logits = sb("logits", [P, GT, ROUTER])
            above = sb("above", [P, GT, ROUTER, ROUTER])
            level = sb("level", [P, GT, ROUTER, ROUTER])
            rank = sb("rank", [P, GT, ROUTER])
            chosen = sb("chosen", [P, GT, ROUTER])
            chosen_logits = sb("chosen_logits", [P, GT, ROUTER])
            pair_sum = sb("pair_sum", [P, GT])
            lead = sb("lead", [P, GT, ROUTER])
            tanh_lead = sb("tanh_lead", [P, GT, ROUTER])
            share = sb("share", [P, GT, ROUTER])
            rs = {name: sem(name) for name in ("router_high router_split logits_made logits_taken logits_turned "
                                               "logits_ready levels_made levels_less levels_masked above_added "
                                               "ranked chosen_set chosen_made sum_made lead_ready tanh_made "
                                               "share_made routed_done").split()}

        def all_steps(eng, body):
            body(0, 0, 0, True, True, True)
            with eng.Fori(1, GROUPS - 1) as g:
                body(0, 0, g, False, True, True)
            body(0, 0, GROUPS - 1, False, True, False)
            if passes > 1:
                with eng.Fori(0, (passes - 1) // 2) as i:
                    for t in range(2):
                        body(2 * i + 1 + t, (1 + t) % 2, 0, True, False, False)
                        with eng.Fori(1, GROUPS) as g:
                            body(2 * i + 1 + t, (1 + t) % 2, g, False, False, False)

        def nothing_before(k, first):
            return first and isinstance(k, int) and k == 0

        def tile(g, t):
            return x[:, GT * g + t, :] if isinstance(g, int) else x[:, bass.ds(GT * g + t, 1), :]

        def flat(ap, g):
            return ap if isinstance(g, int) else ap.unsqueeze(1)

        def cols(buffer, kc, g):
            return buffer[:, kc, g * GROUP:(g + 1) * GROUP] if isinstance(g, int) \
                else buffer[:, kc, bass.ds(g * GROUP, GROUP)]

        block = ctx.enter_context(nc.Block())

        @block.sync
        def _(sp):
            if routed:
                sp.dma_start(router_w[:], dram["router"]).then_inc(router_in, 16)
                sp.dma_start(earlier[:], dram["earlier"]).then_inc(router_in, 16)

            def load(i, c, src):
                sp.wait_ge(s["w_split"], 6 * i + c - 1)
                sp.dma_start(stage[c % 2][:], src).then_inc(piece_in[c % 2], 16)

            for c in range(3):
                if c == 2:
                    sp.wait_ge(s["first_split"], 1)
                sp.dma_start(stage[c % 2][:], weights[c] if passes == 1 else weights[0, c])\
                    .then_inc(piece_in[c % 2], 16)
            if passes > 1:
                with sp.Fori(0, (passes - 1) // 2) as i:
                    for c in range(3, 9):
                        load(i, c, weights[bass.ds(2 * i + c // 3, 1), c % 3, :, :])
            if out is not None:
                rows = out.rearrange("(n b) c t -> (b c) n t", b=2)
                with sp.Fori(0, GROUPS) as g:
                    sp.wait_ge(s["added"], g + 1)
                    sp.dma_start(rows[:, bass.ds(GT * g, GT), :], x[:, bass.ds(GT * g, GT), :]).then_inc(out_stored, 16)
                sp.wait_ge(out_stored, 16 * GROUPS)

        @block.gpsimd
        def _(pool):
            nc.gpsimd.memset(half[:], -0.5).then_inc(s["half_set"], 1)
            pool.wait_ge(s["half_set"], 1)

            def rstd_of(g):
                pool.wait_ge(s["stats_done"], g + 1)
                wait_count(pool, s["xn_ready"], g)
                wait_alone(pool)
                nc.gpsimd.tensor_scalar(var_eps[:].unsqueeze(2), mean_var[:, :, 1:2], EPS, None, ALU.add)\
                    .then_inc(s["eps_added"], 1)
                pool.wait_ge(s["eps_added"], g + 1)
                nc.gpsimd.tensor_tensor(rstd[:], var_eps[:], half[:], ALU.pow).then_inc(s["rstd_ready"], 1)

            def split(i, c):
                k, ring, of = 2 * i + c // 3, c // 3 % RINGS, c % 3
                pool.wait_ge(piece_in[c % 2], 16 * (3 * i + c // 2 + 1))
                pool.wait_ge(s["down_done"], CHUNKS * GROUPS * (k - 1) + 1)
                wait_alone(pool)
                nc.gpsimd.tensor_copy(w_hi[ring][:, of, :], stage[c % 2][:]).then_inc(s["w_high"], 1)
                pool.wait_ge(s["w_high"], 6 * i + c - 2)
                nc.gpsimd.tensor_tensor(w_lo[ring][:, of, :], stage[c % 2][:], w_hi[ring][:, of, :].bitcast(F32),
                                        ALU.subtract).then_inc(s["w_split"], 1)

            rstd_of(0)
            for g in range(1, GROUPS):
                rstd_of(g)
            if passes > 1:
                with pool.Fori(0, (passes - 1) // 2) as i:
                    for c in range(3, 9):
                        split(i, c)

        @block.scalar
        def _(act):
            def high_of(g):
                for kc in range(2):
                    act.wait_ge(s["turned"], 2 * g + kc + 1)
                    nc.scalar.copy(cols(xt_hi, kc, g), t_ps[kc][:]).then_inc(s["hi_taken"], 1)

            def body(k, r, g, first, shared, ahead):
                q = GROUPS * k + g

                def high(m):
                    n = CHUNKS * q + m
                    act.wait_ge(s["product_done"], n + 1)
                    wait_count(act, s["down_done"], n + 1 - CHUNKS)
                    nc.scalar.copy(h_hi[:, m, :], h_all[m % 2][:]).then_inc(s["hi_done"], 1)

                for m in range(CHUNKS):
                    n = CHUNKS * q + m
                    act.wait_ge(s["gate_done"], n + 1)
                    wait_count(act, s["product_done"], n - 1)
                    nc.scalar.activation(silu[m % 2][:], g_ps[m % 2][:], ACT.Silu).then_inc(s["silu_done"], 1)
                    if m == 0 and shared and routed:
                        act.wait_ge(rs["logits_made"], g + 1)
                        wait_count(act, rs["logits_turned"], g)
                        nc.scalar.copy(logits_t[:], t_ps[0][0:ROUTER, :]).then_inc(rs["logits_taken"], 1)
                    if m > 0:
                        high(m - 1)
                    if m == TURN_AT and m < CHUNKS - 1 and ahead:
                        high_of(g + 1)
                high(CHUNKS - 1)
                if TURN_AT == CHUNKS - 1 and ahead:
                    high_of(g + 1)
                if shared and routed:
                    act.wait_ge(rs["lead_ready"], g + 1)
                    nc.scalar.activation(tanh_lead[:], lead[:], ACT.Tanh).then_inc(rs["tanh_made"], 1)

            for c in range(3):
                act.wait_ge(piece_in[c % 2], 16 * (c // 2 + 1))
                nc.scalar.copy(w_hi[0][:, c, :], stage[c % 2][:]).then_inc(s["first_high"], 1)
                if c == 0:
                    high_of(0)
            all_steps(act, body)

        @block.vector
        def _(dve):
            def stats_of(g):
                for t in range(GT):
                    last = nc.vector.bn_stats(stats[:, t, :], tile(g, t))
                last.then_inc(s["stats_raw"], 1)
                dve.wait_ge(s["stats_raw"], g + 1)
                wait_count(dve, s["eps_added"], g)
                wait_count(dve, s["xn_ready"], g)
                wait_alone(dve)
                for t in range(GT):
                    last = nc.vector.bn_aggr(mean_var[:, t, :], stats[:, t, :])
                last.then_inc(s["stats_done"], 1)

            def norm_of(g):
                dve.wait_ge(s["rstd_ready"], g + 1)
                wait_count(dve, s["turned"], 2 * g)
                for t in range(GT):
                    last = nc.vector.tensor_scalar(flat(xn[:, t, :], g), tile(g, t), mean_var[:, t, 0:1],
                                                   rstd[:, t:t + 1], ALU.subtract, ALU.mult)
                last.then_inc(s["xn_ready"], 1)

            def low_of(g):
                for kc in range(2):
                    dve.wait_ge(s["hi_taken"], 2 * g + kc + 1)
                    nc.vector.tensor_tensor(cols(xt_lo, kc, g), t_ps[kc][:], cols(xt_hi, kc, g).bitcast(F32),
                                            ALU.subtract).then_inc(s["lo_taken"], 1)

            if routed:
                dve.wait_ge(router_in, 32)
                nc.vector.tensor_copy(router_hi[:], router_w[:]).then_inc(rs["router_high"], 1)
                dve.wait_ge(rs["router_high"], 1)
                nc.vector.tensor_tensor(router_lo[:], router_w[:], router_hi[:].bitcast(F32), ALU.subtract)\
                    .then_inc(rs["router_split"], 1)
            nc.vector.tensor_copy(combine[:, 0, :], tanh_gain[:, gain_at:gain_at + 1].to_broadcast([P, TILES]))\
                .then_inc(s["shared_set"], 1)
            dve.wait_ge(s["shared_set"], 1)

            def route(g):
                one, two = logits[:].unsqueeze(3), logits[:].unsqueeze(2)
                wide = [P, GT, ROUTER, ROUTER]
                nc.vector.tensor_tensor(above[:], two.to_broadcast(wide), one.to_broadcast(wide), ALU.is_gt)
                nc.vector.tensor_tensor(level[:], two.to_broadcast(wide), one.to_broadcast(wide), ALU.is_ge)\
                    .then_inc(rs["levels_made"], 1)
                dve.wait_ge(rs["levels_made"], g + 1)
                nc.vector.tensor_tensor(level[:], level[:], above[:], ALU.subtract).then_inc(rs["levels_less"], 1)
                dve.wait_ge(rs["levels_less"], g + 1)
                nc.vector.tensor_tensor(level[:].rearrange("p t a b -> p t (a b)"),
                                        level[:].rearrange("p t a b -> p t (a b)"),
                                        earlier[:].rearrange("p a b -> p (a b)").unsqueeze(1)
                                        .to_broadcast([P, GT, ROUTER * ROUTER]), ALU.mult)\
                    .then_inc(rs["levels_masked"], 1)
                dve.wait_ge(rs["levels_masked"], g + 1)
                nc.vector.tensor_tensor(above[:], above[:], level[:], ALU.add).then_inc(rs["above_added"], 1)
                dve.wait_ge(rs["above_added"], g + 1)
                nc.vector.tensor_reduce(rank[:], above[:], AX_X, ALU.add).then_inc(rs["ranked"], 1)
                dve.wait_ge(rs["ranked"], g + 1)
                nc.vector.tensor_scalar(chosen[:], rank[:], 2.0, None, ALU.is_lt).then_inc(rs["chosen_set"], 1)
                dve.wait_ge(rs["chosen_set"], g + 1)
                nc.vector.tensor_tensor(chosen_logits[:], chosen[:], logits[:], ALU.mult).then_inc(rs["chosen_made"], 1)
                dve.wait_ge(rs["chosen_made"], g + 1)
                nc.vector.tensor_reduce(pair_sum[:], chosen_logits[:], AX_X, ALU.add).then_inc(rs["sum_made"], 1)
                dve.wait_ge(rs["sum_made"], g + 1)
                nc.vector.scalar_tensor_tensor(out=lead[:], in0=pair_sum[:].unsqueeze(2).to_broadcast([P, GT, ROUTER]),
                                               scalar=-0.5, in1=logits[:], op0=ALU.mult, op1=ALU.add)\
                    .then_inc(rs["lead_ready"], 1)
                dve.wait_ge(rs["tanh_made"], g + 1)
                nc.vector.scalar_tensor_tensor(out=share[:], in0=tanh_lead[:], scalar=1.0, in1=chosen[:],
                                               op0=ALU.add, op1=ALU.mult).then_inc(rs["share_made"], 1)
                dve.wait_ge(rs["share_made"], g + 1)
                for t in range(GT):
                    at = GT * g + t
                    dst = combine[:, 1:passes, at:at + 1] if isinstance(g, int) else combine[:, 1:passes, bass.ds(at, 1)]
                    last = nc.vector.tensor_scalar(dst, share[:, t, :].unsqueeze(2), tanh_gain[:, gain_at:gain_at + 1],
                                                   0.5, ALU.mult, ALU.mult)
                last.then_inc(rs["routed_done"], 1)

            def add(q, g):
                dve.wait_ge(s["down_done"], CHUNKS * (q + 1))
                dve.wait_ge(s["now_set"], q + 1)
                for t in range(GT):
                    y = flat(y_ps[:, t, :], g)
                    last = nc.vector.scalar_tensor_tensor(out=tile(g, t), in0=y, scalar=now[:, t:t + 1],
                                                          in1=tile(g, t), op0=ALU.mult, op1=ALU.add)
                last.then_inc(s["added"], 1)

            def body(k, r, g, first, shared, ahead):
                q = GROUPS * k + g

                def low(m):
                    n = CHUNKS * q + m
                    dve.wait_ge(s["hi_done"], n + 1)
                    wait_count(dve, s["down_done"], n + 1 - CHUNKS)
                    nc.vector.tensor_tensor(h_lo[:, m, :], h_all[m % 2][:], h_hi[:, m, :].bitcast(F32), ALU.subtract)\
                        .then_inc(s["lo_done"], 1)

                if routed and not shared:
                    dve.wait_ge(rs["routed_done"], GROUPS)
                for m in range(CHUNKS):
                    n = CHUNKS * q + m
                    dve.wait_ge(s["silu_done"], n + 1)
                    dve.wait_ge(s["up_done"], n + 1)
                    wait_count(dve, s["lo_done"], n - 1)
                    nc.vector.tensor_tensor(h_all[m % 2][:], silu[m % 2][:], u_ps[m % 2][:], ALU.mult)\
                        .then_inc(s["product_done"], 1)
                    if m == 0 and ahead:
                        stats_of(g + 1)
                    if m > 0:
                        low(m - 1)
                    if m == 1:
                        if not nothing_before(k, first):
                            add(q - 1, GROUPS - 1 if first else g - 1)
                        weight = combine[:, k, GT * g:GT * g + GT] if isinstance(g, int) and isinstance(k, int) else \
                            combine[:].rearrange("p k t -> p (k t)")[:, bass.ds(k * TILES + GT * g, GT)]
                        wait_count(dve, s["added"], q)
                        nc.vector.tensor_copy(now[:], weight).then_inc(s["now_set"], 1)
                    if m == 1 and ahead:
                        norm_of(g + 1)
                    if m == 2 and shared and routed:
                        dve.wait_ge(rs["logits_turned"], g + 1)
                        nc.vector.tensor_copy(logits[:].rearrange("p t e -> p (t e)"), t_ps[1][:, 0:GT * ROUTER])\
                            .then_inc(rs["logits_ready"], 1)
                    if m == TURN_AT and m < CHUNKS - 1 and ahead:
                        low_of(g + 1)
                low(CHUNKS - 1)
                if TURN_AT == CHUNKS - 1 and ahead:
                    low_of(g + 1)
                if shared and routed:
                    dve.wait_ge(rs["logits_ready"], g + 1)
                    route(g)

            stats_of(0)
            norm_of(0)
            for c in range(3):
                dve.wait_ge(s["first_high"], c + 1)
                low = nc.vector.tensor_tensor(w_lo[0][:, c, :], stage[c % 2][:], w_hi[0][:, c, :].bitcast(F32),
                                              ALU.subtract)
                if c == 2:
                    low.then_inc(s["w_split"], 3)
                else:
                    low.then_inc(s["first_split"], 1)
                if c == 0:
                    low_of(0)
            all_steps(dve, body)
            add(passes * GROUPS - 1, GROUPS - 1)

        @block.tensor
        def _(pe):
            def turn(g):
                pe.wait_ge(s["xn_ready"], g + 1)
                wait_count(pe, s["lo_taken"], 2 * g)
                if routed:
                    wait_count(pe, rs["logits_ready"], g)
                for kc in range(2):
                    for t in range(GT):
                        last = nc.tensor.transpose(t_ps[kc][:, t * P:(t + 1) * P], xn[:, t, kc * P:(kc + 1) * P], ident[:])
                    last.then_inc(s["turned"], 1)

            def down(q, r, m):
                pe.wait_ge(s["lo_done"], CHUNKS * q + m + 1)
                if m == 0:
                    wait_count(pe, s["added"], q)
                for t in range(GT):
                    for a, (h, w) in enumerate(((h_hi, w_hi[r]), (h_hi, w_lo[r]), (h_lo, w_hi[r]))):
                        last = nc.tensor.matmul(y_ps[:, t, :], h[:, m, t * P:(t + 1) * P],
                                                w[:, 2, m * D:(m + 1) * D],
                                                start=(m == 0 and a == 0 and t % 2 == 0),
                                                stop=(m == CHUNKS - 1 and a == 2), skip_group_check=True)
                last.then_inc(s["down_done"], 1)

            def body(k, r, g, first, shared, ahead):
                q = GROUPS * k + g

                def products(m):
                    n = CHUNKS * q + m
                    for bank, base, before, done in ((g_ps, 0, "silu_done", "gate_done"),
                                                     (u_ps, hidden, "product_done", "up_done")):
                        wait_count(pe, s[before], n - 1)
                        at = base + m * P
                        terms = [(w, xt, kc) for kc in range(2) for w, xt in
                                 ((w_hi[r], xt_hi), (w_lo[r], xt_hi), (w_hi[r], xt_lo))]
                        for t, (w, xt, kc) in enumerate(terms):
                            last = nc.tensor.matmul(bank[m % 2][:], w[:, kc, at:at + P], cols(xt, kc, g),
                                                    start=(t == 0), stop=(t == 5))
                        last.then_inc(s[done], 1)

                if nothing_before(k, first):
                    pe.wait_ge(s["first_split"], 2)
                else:
                    pe.wait_ge(s["w_split"], 3 * (k + 1))
                for m in range(CHUNKS):
                    products(m)
                    if m == 0 and shared and routed:
                        for t, (w, xt, kc) in enumerate([(w, xt, kc) for kc in range(2) for w, xt in
                                                         ((router_hi, xt_hi), (router_lo, xt_hi), (router_hi, xt_lo))]):
                            last = nc.tensor.matmul(t_ps[0][0:ROUTER, :], w[:, kc, :], cols(xt, kc, g),
                                                    start=(t == 0), stop=(t == 5))
                        last.then_inc(rs["logits_made"], 1)
                    if m == 1 and shared and routed:
                        pe.wait_ge(rs["logits_taken"], g + 1)
                        wait_alone(pe)
                        for t in range(GT):
                            last = nc.tensor.transpose(t_ps[1][:, t * ROUTER:(t + 1) * ROUTER],
                                                       logits_t[:, t * P:(t + 1) * P], ident[0:ROUTER, 0:ROUTER])
                        last.then_inc(rs["logits_turned"], 1)
                    if m == TURN_AT and ahead:
                        turn(g + 1)
                    if m == 2 and nothing_before(k, first):
                        pe.wait_ge(s["w_split"], 3)
                    if m >= 2:
                        down(q, r, m - 2)
                    elif not nothing_before(k, first):
                        down(q - 1, (r - 1) % RINGS if first else r, CHUNKS - 2 + m)

            turn(0)
            if routed:
                pe.wait_ge(rs["router_split"], 1)
            pe.wait_ge(s["lo_taken"], 2)

            def stepped(k, r, g, first, shared, ahead):
                if shared:
                    pe.wait_ge(s["lo_taken"], 2 * g + 2)
                body(k, r, g, first, shared, ahead)

            all_steps(pe, stepped)
            for m in (CHUNKS - 2, CHUNKS - 1):
                down(passes * GROUPS - 1, (passes - 1) % RINGS, m)


def recurrent_gate(nc, dram, x, ident, tanh_gain, rotated):
    FWHT_CHUNKS = FF2 // P
    RH = 8
    QUARTER = TILES // 4
    with ExitStack() as ctx:
        def sb(name, shape, dt=F32):
            return ctx.enter_context(nc.sbuf_tensor(name, shape, dt))

        def ps(name, shape, dt=F32):
            return ctx.enter_context(nc.psum_tensor(name, shape, dt))

        def sem(name):
            return nc.alloc_semaphore(name)

        w_all = sb("gate_w", [P, 2, 2, P])
        w_hi = sb("gate_w_hi", [P, 2, 2, P], F32R)
        w_lo = sb("gate_w_lo", [P, 2, 2, P], F32R)
        bias = sb("gate_bias", [P, 2, 2])
        half_bias = sb("half_bias", [P, 2, 2])
        ones = sb("gate_ones", [P, 1])
        xn = sb("gate_xn", [P, GT, D])
        stats = sb("gate_stats", [P, GT, 6])
        mean_var = sb("gate_mean_var", [P, GT, 2])
        var_eps = sb("gate_var_eps", [P, GT])
        rstd = sb("gate_rstd", [P, GT])
        half = sb("gate_half", [P, GT])
        xt_hi = [sb(f"gate_xt_hi{r}", [P, 2, GROUP], F32R) for r in range(2)]
        xt_lo = [sb(f"gate_xt_lo{r}", [P, 2, GROUP], F32R) for r in range(2)]
        tanh_x = [sb(f"tanh_x{r}", [P, 2, GROUP]) for r in range(2)]
        tanh_a = sb("tanh_a", [P, 2, GROUP])
        gated = sb("gated", [P, 2, BATCH * CH])
        a_all = sb("a_all", [P, 2, BATCH * CH])
        rest = sb("rest", [P, 2, BATCH * CH])
        shared = sb("shared", [P, TILES * D])
        c_all = shared[:].rearrange("p (n d) -> p n d", d=D)
        rings = shared[:, 0:4 * 2 * GROUP].rearrange("p (n k t) -> p n k t", n=4, k=2)
        from_pool = [rings[:, r, :, :] for r in range(2)]
        y_t = [rings[:, 2 + r, :, :] for r in range(2)]
        w2 = [shared[:, (2 + r) * FWHT_CHUNKS * D:(3 + r) * FWHT_CHUNKS * D].rearrange("p (c d) -> p c d", d=D)
              for r in range(2)]
        hadamard = sb("hadamard", [P, P])
        batch_ones = sb("batch_ones", [P, 32])
        sums = sb("sums", [P, TILES * RH])
        row_max = sb("pool_max", [P, 2, 2])
        shifted = sb("shifted", [P, 2, 2, CH])
        exps = sb("exps", [P, 2, 2, CH])
        total = sb("total", [P, 2, 2])
        attn_t = sb("attn_t", [P, 2, 2, CH])
        attn = sb("attn", [P, TILES * RH])
        pooled = sb("pooled", [P, 2, BATCH])
        decay = sb("decay", [P, 2, 2])
        a_param = sb("a_param", [P, 2])
        positive, magnitude, u, one_more, less, none, logged, ratio, result = \
            (sb("softplus_" + name, [P, 2]) for name in
             "positive magnitude u one_more less none logged ratio result".split())

        t_ps = [ps(f"gate_t_ps{r}", [P, GROUP]) for r in range(2)]
        z_ps = [ps(f"z_ps{r}", [P, 2, GROUP]) for r in range(2)]
        y_ps = [ps(f"gate_y_ps{r}", [P, 2, D]) for r in range(2)]
        pool_ps = [y_ps[h][:, 0, 0:P] for h in range(2)]
        lifted = [c_all[:, r * QUARTER:r * QUARTER + 2, :] for r in range(4)]

        small_in, w2_in, stored = sem("gate_small_in"), sem("w2_in"), sem("rotated_stored")
        param_in = sem("param_in")
        c_all_in = [sem(f"c_all_in{r}") for r in range(4)]
        s = {name: sem("gate_" + name) for name in
             "w_high w_split bias_ready half_set stats_raw stats_done eps_added rstd_ready xn_ready turned hi_taken "
             "all_taken lo_taken z_done tanh_done a_done squared gated_ready rest_ready rooted product_done pool_done "
             "y_ready y_turned x_updated butterflies rotated_done rotated_taken".split()}
        pooling = {name: sem("pool_" + name) for name in
                   "summed turned maxed shifted_done exp_done totalled inverted attn_done turned_back attn_taken "
                   "weighted added_up lifted lifted_turned taken softplus_step".split()}
        block = ctx.enter_context(nc.Block())

        def by_pairs(eng, body, after_two=None):
            for g in range(2):
                body(g, g)
            if after_two:
                after_two()
            with eng.Fori(1, GROUPS // 2) as i:
                for r in range(2):
                    body(2 * i + r, r)

        def steps(eng, body, after_second=None, after_loop=None, after_seventh=None):
            body(0, 0, True)
            body(1, 1, True)
            if after_second:
                after_second()
            with eng.Fori(1, GROUPS // 2 - 1) as i:
                for r in range(2):
                    body(2 * i + r, r, True)
            if after_loop:
                after_loop()
            body(GROUPS - 2, 0, False)
            if after_seventh:
                after_seventh()
            body(GROUPS - 1, 1, False)

        def there(g, k):
            return not isinstance(g, int) or 0 <= g + k < GROUPS

        def cols(buffer, g):
            return buffer[:, :, g * GROUP:(g + 1) * GROUP] if isinstance(g, int) \
                else buffer[:, :, bass.ds(g * GROUP, GROUP)]

        def col(buffer, kc, g):
            return buffer[:, kc, g * GROUP:(g + 1) * GROUP] if isinstance(g, int) \
                else buffer[:, kc, bass.ds(g * GROUP, GROUP)]

        def tile(g, t):
            return x[:, GT * g + t, :] if isinstance(g, int) else x[:, bass.ds(GT * g + t, 1), :]

        def flat(ap, g):
            return ap if isinstance(g, int) else ap.unsqueeze(1)

        @block.sync
        def _(sp):
            rows = dram["ctx_2048"][0:BATCH, :, :].rearrange("(n b) c t -> (b c) n t", b=2)
            sp.dma_start(a_param[:], dram["a_param"]).then_inc(param_in, 16)
            sp.dma_start(w_all[:], dram["gate_blocks"]).then_inc(small_in, 16)
            sp.dma_start(bias[:], dram["gate_bias"]).then_inc(small_in, 16)
            sp.dma_start(batch_ones[:], dram["batch_ones"]).then_inc(small_in, 16)
            sp.dma_start(hadamard[:], dram["hadamard"]).then_inc(small_in, 16)
            for r in range(4):
                sp.dma_start(c_all[:, r * QUARTER:(r + 1) * QUARTER, :], rows[:, r * QUARTER:(r + 1) * QUARTER, :])\
                    .then_inc(c_all_in[r], 16)
            sp.wait_ge(pooling["taken"], 4)
            sp.dma_start(w2[0], dram["w2_rows"]).then_inc(w2_in, 16)
            sp.wait_ge(s["rotated_taken"], 4)
            sp.dma_start(rotated, w2[0].rearrange("p c d -> p (c d)")).then_inc(stored, 16)
            sp.wait_ge(stored, 16)

        @block.gpsimd
        def _(pool):
            nc.gpsimd.memset(half[:], -0.5).then_inc(s["half_set"], 1)
            pool.wait_ge(s["half_set"], 1)

            def rstd_of(g):
                pool.wait_ge(s["stats_done"], g + 1)
                wait_count(pool, s["xn_ready"], g)
                wait_alone(pool)
                nc.gpsimd.tensor_scalar(var_eps[:].unsqueeze(2), mean_var[:, :, 1:2], EPS, None, ALU.add)\
                    .then_inc(s["eps_added"], 1)
                pool.wait_ge(s["eps_added"], g + 1)
                nc.gpsimd.tensor_tensor(rstd[:], var_eps[:], half[:], ALU.pow).then_inc(s["rstd_ready"], 1)

            rstd_of(0)
            with pool.Fori(1, GROUPS) as g:
                rstd_of(g)

            def scale_pooled(g, r):
                wait_count(pool, s["y_ready"], g - 1)
                for kc in range(2):
                    at = bass.ds(g * (GROUP // CH), GROUP // CH)
                    last = nc.gpsimd.tensor_tensor(
                        from_pool[r][:, kc, :].rearrange("p (b t) -> p b t", t=CH),
                        col(a_all, kc, g).rearrange("p (b t) -> p b t", t=CH),
                        pooled[:, kc, at].unsqueeze(2).to_broadcast([P, GROUP // CH, CH]), ALU.mult)
                last.then_inc(s["pool_done"], 1)

            pool.wait_ge(pooling["taken"], 4)
            pool.wait_ge(s["a_done"], 2 * GROUPS)
            by_pairs(pool, scale_pooled)

        @block.vector
        def _(dve):
            def stats_of(g):
                for t in range(GT):
                    last = nc.vector.bn_stats(stats[:, t, :], tile(g, t))
                last.then_inc(s["stats_raw"], 1)
                dve.wait_ge(s["stats_raw"], g + 1)
                wait_count(dve, s["eps_added"], g)
                wait_count(dve, s["xn_ready"], g)
                wait_alone(dve)
                for t in range(GT):
                    last = nc.vector.bn_aggr(mean_var[:, t, :], stats[:, t, :])
                last.then_inc(s["stats_done"], 1)

            def norm_of(g):
                dve.wait_ge(s["rstd_ready"], g + 1)
                wait_count(dve, s["turned"], 2 * g)
                for t in range(GT):
                    last = nc.vector.tensor_scalar(flat(xn[:, t, :], g), tile(g, t), mean_var[:, t, 0:1],
                                                   rstd[:, t:t + 1], ALU.subtract, ALU.mult)
                last.then_inc(s["xn_ready"], 1)

            def low_of(g, r):
                wait_count(dve, s["z_done"], 2 * g - 2)
                for kc in range(2):
                    dve.wait_ge(s["all_taken"], 2 * g + kc + 1)
                    nc.vector.tensor_tensor(xt_lo[r][:, kc, :], col(gated, kc, g), xt_hi[r][:, kc, :].bitcast(F32),
                                            ALU.subtract).then_inc(s["lo_taken"], 1)

            def use(g, r):
                dve.wait_ge(s["tanh_done"], 2 * g + 2)
                dve.wait_ge(s["lo_taken"], 2 * g + 2)
                nc.vector.scalar_tensor_tensor(out=cols(gated, g), in0=tanh_x[r][:], scalar=1.0, in1=cols(gated, g),
                                               op0=ALU.add, op1=ALU.mult).then_inc(s["gated_ready"], 1)
                dve.wait_ge(s["squared"], 2 * g + 2)
                nc.vector.tensor_scalar(cols(rest, g), cols(rest, g), 1.0, None, ALU.min).then_inc(s["rest_ready"], 1)

            def body(g, r, ahead):
                if ahead:
                    stats_of(g + 2)
                if there(g, 1):
                    low_of(g + 1, 1 - r)
                if ahead:
                    norm_of(g + 2)
                if there(g, -1):
                    use(g - 1, 1 - r)

            def softmax():
                for r in range(4):
                    dve.wait_ge(c_all_in[r], 16)
                    nc.vector.tensor_reduce(sums[:, r * QUARTER * RH:(r + 1) * QUARTER * RH],
                                            c_all[:, r * QUARTER:(r + 1) * QUARTER, :]
                                            .rearrange("p n (h d) -> p (n h) d", h=RH), AX_X, ALU.add)\
                        .then_inc(pooling["summed"], 1)
                dve.wait_ge(pooling["turned"], 2)
                for h in range(2):
                    last = nc.vector.tensor_reduce(row_max[:, h, :], pool_ps[h].rearrange("p (b t) -> p b t", b=2),
                                                   AX_X, ALU.max)
                last.then_inc(pooling["maxed"], 1)
                dve.wait_ge(pooling["maxed"], 1)
                for h in range(2):
                    last = nc.vector.tensor_tensor(shifted[:, h, :, :], pool_ps[h].rearrange("p (b t) -> p b t", b=2),
                                                   row_max[:, h, :].unsqueeze(2).to_broadcast([P, 2, CH]), ALU.subtract)
                last.then_inc(pooling["shifted_done"], 1)
                dve.wait_ge(pooling["exp_done"], 1)
                nc.vector.tensor_reduce(total[:], exps[:], AX_X, ALU.add).then_inc(pooling["totalled"], 1)
                dve.wait_ge(pooling["totalled"], 1)
                nc.vector.reciprocal(row_max[:], total[:]).then_inc(pooling["inverted"], 1)
                dve.wait_ge(pooling["inverted"], 1)
                nc.vector.tensor_tensor(attn_t[:], exps[:], row_max[:].unsqueeze(3).to_broadcast([P, 2, 2, CH]),
                                        ALU.mult).then_inc(pooling["attn_done"], 1)

            def take_weights():
                dve.wait_ge(pooling["turned_back"], 2)
                for h in range(2):
                    last = nc.vector.tensor_copy(attn[:, h * P:(h + 1) * P], pool_ps[h])
                last.then_inc(pooling["attn_taken"], 1)
                dve.wait_ge(pooling["attn_taken"], 1)

            def weigh(quarters):
                for r in quarters:
                    part = c_all[:, r * QUARTER:(r + 1) * QUARTER, :].rearrange("p n (h d) -> p (n h) d", h=RH)
                    nc.vector.tensor_tensor(part, part, attn[:, r * QUARTER * RH:(r + 1) * QUARTER * RH].unsqueeze(2)
                                            .to_broadcast([P, QUARTER * RH, D // RH]), ALU.mult)\
                        .then_inc(pooling["weighted"], 1)

            stats_of(0)
            norm_of(0)

            dve.wait_ge(param_in, 16)
            nc.vector.tensor_scalar(positive[:], a_param[:], 0.0, None, ALU.max).then_inc(pooling["softplus_step"], 1)
            dve.wait_ge(pooling["softplus_step"], 1)
            nc.vector.scalar_tensor_tensor(out=magnitude[:], in0=a_param[:], scalar=-1.0, in1=a_param[:],
                                           op0=ALU.mult, op1=ALU.max).then_inc(pooling["softplus_step"], 1)
            dve.wait_ge(pooling["softplus_step"], 3)
            nc.vector.tensor_scalar(one_more[:], u[:], 1.0, None, ALU.add).then_inc(pooling["softplus_step"], 1)
            dve.wait_ge(pooling["softplus_step"], 4)
            nc.vector.tensor_scalar(less[:], one_more[:], -1.0, None, ALU.add).then_inc(pooling["softplus_step"], 1)
            dve.wait_ge(pooling["softplus_step"], 5)
            nc.vector.tensor_scalar(none[:], less[:], 0.0, None, ALU.is_equal).then_inc(pooling["softplus_step"], 1)
            dve.wait_ge(pooling["softplus_step"], 7)
            nc.vector.tensor_tensor(less[:], less[:], none[:], ALU.add).then_inc(pooling["softplus_step"], 1)
            dve.wait_ge(pooling["softplus_step"], 8)
            nc.vector.reciprocal(ratio[:], less[:]).then_inc(pooling["softplus_step"], 1)
            dve.wait_ge(pooling["softplus_step"], 9)
            nc.vector.tensor_tensor(ratio[:], ratio[:], u[:], ALU.mult).then_inc(pooling["softplus_step"], 1)
            dve.wait_ge(pooling["softplus_step"], 10)
            nc.vector.tensor_tensor(ratio[:], ratio[:], logged[:], ALU.mult).then_inc(pooling["softplus_step"], 1)
            dve.wait_ge(pooling["softplus_step"], 11)
            nc.vector.tensor_tensor(result[:], none[:], u[:], ALU.mult).then_inc(pooling["softplus_step"], 1)
            dve.wait_ge(pooling["softplus_step"], 12)
            nc.vector.tensor_tensor(ratio[:], ratio[:], result[:], ALU.add).then_inc(pooling["softplus_step"], 1)
            dve.wait_ge(pooling["softplus_step"], 13)
            nc.vector.tensor_tensor(result[:], ratio[:], positive[:], ALU.add).then_inc(pooling["softplus_step"], 1)
            dve.wait_ge(pooling["softplus_step"], 14)
            nc.vector.tensor_scalar(decay[:, 0, :], result[:], -8.0, None, ALU.mult).then_inc(pooling["softplus_step"], 1)
            dve.wait_ge(pooling["softplus_step"], 15)
            nc.vector.tensor_scalar(decay[:, 1, :], result[:], -4.0, None, ALU.mult).then_inc(pooling["softplus_step"], 1)

            dve.wait_ge(small_in, 64)
            nc.vector.memset(ones[:], 1.0)
            nc.vector.tensor_scalar(half_bias[:], bias[:], 0.5, None, ALU.mult).then_inc(s["bias_ready"], 1)
            nc.vector.tensor_copy(w_hi[:], w_all[:]).then_inc(s["w_high"], 1)
            dve.wait_ge(s["w_high"], 1)
            nc.vector.tensor_tensor(w_lo[:], w_all[:], w_hi[:].bitcast(F32), ALU.subtract).then_inc(s["w_split"], 1)
            stats_of(1)
            low_of(0, 0)
            norm_of(1)
            def lift(quarters):
                for r in quarters:
                    dve.wait_ge(pooling["added_up"], r + 1)
                    nc.vector.tensor_copy(lifted[r], y_ps[r % 2][:]).then_inc(pooling["lifted"], 1)

            def place(quarters):
                for r in quarters:
                    dve.wait_ge(pooling["lifted_turned"], r + 1)
                    for a in range(2):
                        per = 2 * QUARTER
                        last = nc.vector.tensor_copy(
                            pooled[:, :, r * per:(r + 1) * per].rearrange("p h (j a b) -> p h j a b", a=2, b=2)[:, :, :, a, :],
                            y_ps[r % 2][:, a, :].rearrange("p (h j q) -> p h j q", h=2, j=4)[:, :, :, 0:2])
                    last.then_inc(pooling["taken"], 1)

            steps(dve, body, lambda: (softmax(), take_weights()), lambda: (weigh((0, 1)), lift((0, 1))),
                  lambda: (place((0, 1)), weigh((2, 3))))
            lift((2, 3))
            place((2, 3))
            use(GROUPS - 1, 1)

            def transform():
                dve.wait_ge(w2_in, 16)
                for n, span in enumerate((1, 2, 4)):
                    src = w2[n % 2].rearrange("p (a two b) d -> p a two (b d)", two=2, b=span)
                    dst = w2[1 - n % 2].rearrange("p (a two b) d -> p a two (b d)", two=2, b=span)
                    for k, op in enumerate((ALU.add, ALU.subtract)):
                        last = nc.vector.tensor_tensor(dst[:, :, k, :], src[:, :, 0, :], src[:, :, 1, :], op)
                    last.then_inc(s["butterflies"], 1)
                    dve.wait_ge(s["butterflies"], n + 1)

            def make_y(g, r):
                dve.wait_ge(s["rooted"], g + 1)
                wait_count(dve, s["y_turned"], 2 * g - 2)
                nc.vector.scalar_tensor_tensor(out=y_t[r], in0=cols(gated, g), scalar=0.5, in1=cols(rest, g),
                                               op0=ALU.mult, op1=ALU.mult).then_inc(s["product_done"], 1)
                dve.wait_ge(s["product_done"], g + 1)
                dve.wait_ge(s["pool_done"], g + 1)
                nc.vector.tensor_tensor(y_t[r], y_t[r], from_pool[r], ALU.add).then_inc(s["y_ready"], 1)

            def update(g):
                for t in range(2):
                    dve.wait_ge(s["y_turned"], 2 * g + t + 1)
                    rows = x[:, bass.ds(GT * g + 2 * t, 2), :]
                    nc.vector.scalar_tensor_tensor(out=rows, in0=y_ps[t][:], scalar=tanh_gain[:, 2:3], in1=rows,
                                                   op0=ALU.mult, op1=ALU.add).then_inc(s["x_updated"], 1)

            def finish(g, r):
                make_y(g, r)
                if there(g, -1):
                    update(g - 1)

            dve.wait_ge(s["gated_ready"], GROUPS)
            by_pairs(dve, finish, transform)
            update(GROUPS - 1)

        @block.scalar
        def _(act):
            act.wait_ge(param_in, 16)
            act.wait_ge(pooling["softplus_step"], 2)
            nc.scalar.activation(u[:], magnitude[:], ACT.Exp, scale=-1.0).then_inc(pooling["softplus_step"], 1)
            act.wait_ge(pooling["softplus_step"], 6)
            nc.scalar.activation(logged[:], one_more[:], ACT.Ln).then_inc(pooling["softplus_step"], 1)

            def take(g, r):
                wait_count(act, s["z_done"], 2 * g - 2)
                for kc in range(2):
                    act.wait_ge(s["turned"], 2 * g + kc + 1)
                    nc.scalar.copy(xt_hi[r][:, kc, :], t_ps[kc][:]).then_inc(s["hi_taken"], 1)
                    nc.scalar.copy(col(gated, kc, g), t_ps[kc][:]).then_inc(s["all_taken"], 1)

            def gates(g, r):
                for kc in range(2):
                    act.wait_ge(s["z_done"], 2 * g + kc + 1)
                    if kc == 0:
                        wait_count(act, s["gated_ready"], g - 1)
                        wait_count(act, s["squared"], 2 * g)
                    nc.scalar.activation(tanh_a[:, kc, :], z_ps[kc][:, 1, :], ACT.Tanh, bias=half_bias[:, kc, 1:2],
                                         scale=0.5)
                    nc.scalar.activation(tanh_x[r][:, kc, :], z_ps[kc][:, 0, :], ACT.Tanh,
                                         bias=half_bias[:, kc, 0:1], scale=0.5).then_inc(s["tanh_done"], 1)
                act.wait_ge(s["tanh_done"], 2 * g + 2)
                for kc in range(2):
                    nc.scalar.activation(col(a_all, kc, g), tanh_a[:, kc, :], ACT.Exp, bias=decay[:, 1, kc:kc + 1],
                                         scale=decay[:, 1, kc:kc + 1]).then_inc(s["a_done"], 1)
                    nc.scalar.activation(col(rest, kc, g), tanh_a[:, kc, :], ACT.Exp, bias=decay[:, 0, kc:kc + 1],
                                         scale=decay[:, 0, kc:kc + 1]).then_inc(s["squared"], 1)

            def body(g, r, ahead):
                if there(g, 1):
                    take(g + 1, 1 - r)
                gates(g, r)

            def exponentials():
                act.wait_ge(pooling["shifted_done"], 1)
                nc.scalar.activation(exps[:], shifted[:], ACT.Exp, scale=RH / D).then_inc(pooling["exp_done"], 1)

            act.wait_ge(s["bias_ready"], 1)
            take(0, 0)
            act.wait_ge(pooling["softplus_step"], 16)
            steps(act, body, exponentials)
            act.wait_ge(s["rest_ready"], GROUPS)

            def root(g):
                nc.scalar.activation(cols(rest, g), cols(rest, g), ACT.Sqrt, bias=ones[:], scale=-1.0)\
                    .then_inc(s["rooted"], 1)

            root(0)
            with act.Fori(1, GROUPS) as g:
                root(g)
            for n in range(4):
                act.wait_ge(s["rotated_done"], n + 1)
                nc.scalar.mul(w2[0][:, 2 * n:2 * n + 2, :], t_ps[n % 2][:].rearrange("p (c d) -> p c d", c=2),
                              float(FF2) ** -0.5).then_inc(s["rotated_taken"], 1)

        @block.tensor
        def _(pe):
            def turn(g):
                pe.wait_ge(s["xn_ready"], g + 1)
                wait_count(pe, s["all_taken"], 2 * g)
                for kc in range(2):
                    for t in range(GT):
                        last = nc.tensor.transpose(t_ps[kc][:, t * P:(t + 1) * P], xn[:, t, kc * P:(kc + 1) * P], ident[:])
                    last.then_inc(s["turned"], 1)

            def body(g, r, ahead):
                if there(g, 1):
                    turn(g + 1)
                for kc in range(2):
                    pe.wait_ge(s["lo_taken"], 2 * g + kc + 1)
                    wait_count(pe, s["tanh_done"], 2 * g)
                    for gate in range(2):
                        for t, (w, xt) in enumerate(((w_hi, xt_hi[r]), (w_lo, xt_hi[r]), (w_hi, xt_lo[r]))):
                            last = nc.tensor.matmul(z_ps[kc][:, gate, :], w[:, kc, gate, :], xt[:, kc, :],
                                                    start=(t == 0), stop=(t == 2))
                    last.then_inc(s["z_done"], 1)

            def turn_sums():
                for h in range(2):
                    pe.wait_ge(pooling["summed"], 2 * h + 2)
                    nc.tensor.transpose(pool_ps[h], sums[:, h * P:(h + 1) * P], ident[:]).then_inc(pooling["turned"], 1)

            def turn_weights():
                pe.wait_ge(pooling["attn_done"], 1)
                for h in range(2):
                    nc.tensor.transpose(pool_ps[h], attn_t[:, h, :, :], ident[:]).then_inc(pooling["turned_back"], 1)

            def add_up(quarters):
                for r in quarters:
                    pe.wait_ge(pooling["weighted"], r + 1)
                    wait_count(pe, pooling["taken"], r - 1)
                    for j in range(4):
                        at = r * QUARTER + 2 * j
                        last = nc.tensor.matmul(y_ps[r % 2][32 * j:32 * j + 32, :, :], batch_ones[:],
                                                c_all[:, at:at + 2, :], start=True, stop=True)
                    last.then_inc(pooling["added_up"], 1)

            def turn_lifted(quarters):
                for r in quarters:
                    pe.wait_ge(pooling["lifted"], r + 1)
                    for a in range(2):
                        for h in range(2):
                            last = nc.tensor.transpose(y_ps[r % 2][:, a, h * P:(h + 1) * P],
                                                       lifted[r][:, a, h * P:(h + 1) * P], ident[:])
                    last.then_inc(pooling["lifted_turned"], 1)

            turn(0)
            pe.wait_ge(s["w_split"], 1)
            steps(pe, body, lambda: (turn_sums(), turn_weights()), lambda: add_up((0, 1)), lambda: turn_lifted((0, 1)))
            add_up((2, 3))
            turn_lifted((2, 3))
            def transform():
                pe.wait_ge(s["butterflies"], 3)
                pe.wait_ge(s["all_taken"], 2 * GROUPS)
                for n in range(4):
                    wait_count(pe, s["rotated_taken"], n - 1)
                    nc.tensor.matmul(t_ps[n % 2][:], hadamard[:], w2[1][:, 2 * n:2 * n + 2, :].rearrange("p c d -> p (c d)"),
                                     start=True, stop=True).then_inc(s["rotated_done"], 1)

            def turn_back(g, r):
                pe.wait_ge(s["y_ready"], g + 1)
                if isinstance(g, int) and g == 0:
                    pe.wait_ge(pooling["taken"], 4)
                for t in range(2):
                    wait_count(pe, s["x_updated"], 2 * g + t - 1)
                    for a in range(2):
                        for kc in range(2):
                            at = (2 * t + a) * P
                            last = nc.tensor.transpose(y_ps[t][:, a, kc * P:(kc + 1) * P],
                                                       y_t[r][:, kc, at:at + P], ident[:])
                    last.then_inc(s["y_turned"], 1)

            by_pairs(pe, turn_back, transform)


def program(nc, dram, out):
    with ExitStack() as ctx:
        x = ctx.enter_context(nc.sbuf_tensor("x_sb", [P, TILES, D], F32))
        ident = ctx.enter_context(nc.sbuf_tensor("ident", [P, P], F32))
        tanh_gain = ctx.enter_context(nc.sbuf_tensor("tanh_gain", [P, 4], F32))
        rotated = nc.dram_tensor("rotated", (P, FF2 // P * D), F32, kind="Internal").ap()
        with nc.cleanup_on_exit():
            attention(nc, dram, x, ident, tanh_gain)
        with nc.cleanup_on_exit():
            feed_forward(nc, dram, x, ident, tanh_gain, 1, FF, EXPERTS + 1, dram["experts"], True)
        with nc.cleanup_on_exit():
            recurrent_gate(nc, dram, x, ident, tanh_gain, rotated)
        feed_forward(nc, dram, x, ident, tanh_gain, 3, FF2, 1, [dram["w13"][0], dram["w13"][1], rotated], False, out)


def layouts(a):
    a = {name: np.asarray(v) for name, v in a.items()}
    batch_of, ch_of, d_of = column_order()
    swap = ch_of - d_of + np.where(d_of < 4, d_of ^ 2, d_of)

    def per_batch(w_t, cols, batch):
        w = np.zeros((2, CH, P), np.float32)
        for b in range(2):
            w[b][:, batch == b] = w_t[:, cols[batch == b]]
        return w.reshape(P, P)

    plain, plain_batch = np.tile(np.arange(CH), 2), np.repeat(np.arange(2), CH)
    wq, wk, wv, wo = (a[f"L0_xattn_W{m}"].T for m in "qkvo")
    bq, bk, bv, bo = (a[f"L0_xattn_b{m}"] for m in "qkvo")
    own = np.zeros((P, UH), np.float32)
    own[96 + np.arange(8), np.arange(8) % UH] = 1
    out = {
        "x": a["x"],
        "ctx_2048": np.concatenate([a["ctx_2048"], np.zeros((2, CH, D), np.float32)]),
        "ident": np.eye(P, dtype=np.float32),
        "w_in": np.stack([per_batch(wq, ch_of, batch_of), per_batch(wq, swap, batch_of),
                          per_batch(wk, ch_of, batch_of), per_batch(wk, swap, batch_of),
                          per_batch(wv, plain, plain_batch)], 1),
        "w_out": per_batch(wo, plain, plain_batch),
        "bias": np.stack([bq[ch_of], bq[swap], bk[ch_of], bk[swap], bo[plain]], 1),
        "bias_v": np.broadcast_to(bv[plain], (P, P)),
        "rope": np.stack(rotary_tables(), 1),
        "own_head": own,
        "gains": np.broadcast_to(np.stack([a["g_xattn"][0], a["g_ffn"][0], a["g_xattn"][1], a["g_ffn"][1]]), (P, 4)),
    }

    def pieces(gate_up, down):
        return np.concatenate([gate_up.reshape(2, P, -1),
                               down.reshape(-1, P, D).transpose(1, 0, 2).reshape(1, P, -1)])

    gate_up = [a["L0_ffn_shared_gate_up"], *a["L0_ffn_w_gate_up"]]
    down = [a["L0_ffn_shared_down"], *a["L0_ffn_w_down"]]
    out["experts"] = np.stack([pieces(g, d) for g, d in zip(gate_up, down)])
    out["w13"] = np.concatenate([a["L1_ffn_W1"].T, a["L1_ffn_W3"].T], 1).reshape(2, P, 2 * FF2)
    out["w2_rows"] = a["L1_ffn_W2"].T.reshape(FF2 // P, P, D).transpose(1, 0, 2)
    hadamard = np.ones((1, 1), np.float32)
    while len(hadamard) < P:
        hadamard = np.block([[hadamard, hadamard], [hadamard, -hadamard]])
    out["hadamard"] = hadamard
    blocks = np.zeros((2, P, 2, P), np.float32)
    for gate, w in enumerate((a["L1_xattn_w_input"], a["L1_xattn_w_a"])):
        for h in range(8):
            at = h % 4 * 32
            blocks[h // 4, at:at + 32, gate, at:at + 32] = w[h]
    out["gate_blocks"] = blocks.transpose(1, 0, 2, 3)
    out["gate_bias"] = np.stack([a["L1_xattn_b_input"].reshape(2, P), a["L1_xattn_b_a"].reshape(2, P)], 1).transpose(2, 0, 1)
    out["a_param"] = a["L1_xattn_a_param"].reshape(2, P).T
    out["batch_ones"] = np.repeat(np.eye(2, 32, dtype=np.float32), CH, 0)
    out["router"] = a["L0_ffn_gate_w"].reshape(2, P, EXPERTS).transpose(1, 0, 2)
    out["earlier"] = np.broadcast_to(np.tril(np.ones((EXPERTS, EXPERTS), np.float32), -1), (P, EXPERTS, EXPERTS))
    return {name: np.ascontiguousarray(v) for name, v in out.items()}


def kernel(**inputs):
    import concourse.bacc as bacc
    from concourse.bass_utils import run_bass_kernel_spmd

    arrays = layouts(inputs)
    nc = bacc.Bacc("TRN2", target_bir_lowering=False, num_devices=1)
    dram = {name: nc.dram_tensor(f"in_{name}", v.shape, mybir.dt.from_np(v.dtype), kind="ExternalInput").ap()
            for name, v in arrays.items()}
    out = nc.dram_tensor("out", (BATCH, CH, D), F32, kind="ExternalOutput").ap()
    program(nc, dram, out)
    done = run_bass_kernel_spmd(nc, [{f"in_{name}": v for name, v in arrays.items()}], core_ids=[0])
    return done.results[0]["out"]
```
